# Optimizing a Trainium2 kernel written in Bass

```python
import numpy as np
import jax
import jax.numpy as jnp

def _softmax(x, axis=-1):
    return jax.nn.softmax(x, axis=axis)

def _gelu(x):
    return jax.nn.gelu(x, approximate=True)

def _silu(x):
    return jax.nn.silu(x)

def _sigmoid(x):
    return jax.nn.sigmoid(x)

def _layernorm(x, axis=-1, eps=1e-05):
    m = jnp.mean(x, axis=axis, keepdims=True)
    v = jnp.var(x, axis=axis, keepdims=True)
    return (x - m) / jnp.sqrt(v + eps)

def _scatter_add(tgt, idx, src, axis=0):
    return tgt.at[idx].add(src)

def _segment_sum(src, seg, n):
    return jax.ops.segment_sum(src, seg, n)
kernel_name = 'mk_gnn_ffn_d1_gnn_r8_46363d'

def setup_inputs(seed: int=0):
    np.random.seed(seed)
    _w = jnp.asarray

    def _rec_inputs():
        import jax
        import jax.numpy as jnp
        _gk = jax.random.key(seed)
        x = -0.0003713 + 1 * jax.random.normal(jax.random.fold_in(_gk, 1), (6250, 256), jnp.float32)
        src = jax.random.randint(jax.random.fold_in(_gk, 2), (100000,), 0, 6250, jnp.int32)
        dst = jnp.minimum((6250 * jax.random.uniform(jax.random.fold_in(_gk, 3), (100000,)) ** 2.0).astype(jnp.int32), 49999)
        _o = jnp.argsort(dst, stable=True)
        src = src[_o]
        dst = dst[_o]
        edge_weight = jax.random.uniform(jax.random.fold_in(_gk, 12), (100000,), jnp.float32, 0.0, 0.999998)
        return (x, src, dst, edge_weight)
    x, src, dst, edge_weight = _rec_inputs()

    def _L0_gnn_setup():
        import jax, jax.numpy as jnp
        import numpy as np
        N_NODES = 6250
        N_EDGES = 100000
        D_IN = 256
        D_OUT = 256
        key = jax.random.key(seed)
        k1, k2, k3, k4, k5 = jax.random.split(key, 5)
        inp = {'input': jax.random.normal(k1, (N_NODES, D_IN), dtype=jnp.float32), 'edge_index': jax.random.randint(k2, (2, N_EDGES), 0, N_NODES, dtype=jnp.int64), 'edge_attr': jax.random.uniform(k3, (N_EDGES,), dtype=jnp.float32), 'W_weight': jax.random.normal(k4, (D_OUT, D_IN), dtype=jnp.float32) / np.sqrt(D_IN), 'W_bias': jax.random.normal(k5, (D_OUT,), dtype=jnp.float32) * 0.01}
        return inp
    _L0_gnn_all = _L0_gnn_setup()
    _L0_gnn_in = {k: v for k, v in _L0_gnn_all.items() if k in ('W_weight', 'W_bias')}
    del _L0_gnn_all

    def _L0_ffn_setup():
        import jax, jax.numpy as jnp
        import numpy as np
        B, T, D, H, L = (16, 512, 256, 256, 2)

        def _lstm(x, W_ih, W_hh, b_ih, b_hh):
            x_proj = jnp.einsum('btd,gd->btg', x, W_ih) + b_ih + b_hh
            h0 = jnp.zeros((x.shape[0], W_hh.shape[1]), x.dtype)
            c0 = jnp.zeros_like(h0)

            def step(carry, xp):
                h, c = carry
                gates = xp + h @ W_hh.T
                i, f, g, o = jnp.split(gates, 4, axis=-1)
                c = jax.nn.sigmoid(f) * c + jax.nn.sigmoid(i) * jnp.tanh(g)
                h = jax.nn.sigmoid(o) * jnp.tanh(c)
                return ((h, c), h)
            _, hs = jax.lax.scan(step, (h0, c0), jnp.swapaxes(x_proj, 0, 1))
            return jnp.swapaxes(hs, 0, 1)
        key = jax.random.key(seed)
        ks = jax.random.split(key, 9)
        s = 1.0 / np.sqrt(H)
        u = lambda k, shape: jax.random.uniform(k, shape, jnp.float32, -s, s)
        return {'x': jax.random.normal(ks[0], (B, T, D), jnp.float32), 'W_ih': u(ks[1], (4 * H, D)), 'W_hh': u(ks[2], (4 * H, H)), 'b_ih': u(ks[3], (4 * H,)), 'b_hh': u(ks[4], (4 * H,)), 'W_lin': u(ks[5], (L, H)), 'b_lin': u(ks[6], (L,)), 'fw_att': jnp.full((1, H), 0.001, jnp.float32), 'bw_att': jnp.full((1, H), 0.001, jnp.float32)}
    _L0_ffn_all = _L0_ffn_setup()
    _L0_ffn_in = {k: v for k, v in _L0_ffn_all.items() if k in ('W_ih', 'W_hh', 'b_ih', 'b_hh', 'W_lin', 'b_lin', 'fw_att', 'bw_att')}
    del _L0_ffn_all
    return {'x': x, 'src': src, 'dst': dst, 'edge_weight': edge_weight, 'L0_gnn_W_weight': _L0_gnn_in['W_weight'], 'L0_gnn_W_bias': _L0_gnn_in['W_bias'], 'L0_ffn_W_ih': _L0_ffn_in['W_ih'], 'L0_ffn_W_hh': _L0_ffn_in['W_hh'], 'L0_ffn_b_ih': _L0_ffn_in['b_ih'], 'L0_ffn_b_hh': _L0_ffn_in['b_hh'], 'L0_ffn_W_lin': _L0_ffn_in['W_lin'], 'L0_ffn_b_lin': _L0_ffn_in['b_lin'], 'L0_ffn_fw_att': _L0_ffn_in['fw_att'], 'L0_ffn_bw_att': _L0_ffn_in['bw_att']}

def reference(x, src, dst, edge_weight, L0_gnn_W_weight, L0_gnn_W_bias, L0_ffn_W_ih, L0_ffn_W_hh, L0_ffn_b_ih, L0_ffn_b_hh, L0_ffn_W_lin, L0_ffn_b_lin, L0_ffn_fw_att, L0_ffn_bw_att):
    import jax
    import jax.numpy as jnp

    def _L0_gnn_ref(input, edge_index, edge_attr, W_weight, W_bias):
        import jax, jax.numpy as jnp
        import numpy as np
        N_NODES = 6250
        N_EDGES = 100000
        D_IN = 256
        D_OUT = 256
        support = jnp.einsum('ni,oi->no', input, W_weight) + W_bias
        row, col = (edge_index[0], edge_index[1])
        messages = support[col] * edge_attr[:, None]
        output = jax.ops.segment_sum(messages, row, num_segments=N_NODES)
        return output

    def _L0_ffn_ref(x, W_ih, W_hh, b_ih, b_hh, W_lin, b_lin, fw_att, bw_att):
        import jax, jax.numpy as jnp
        import numpy as np
        B, T, D, H, L = (16, 512, 256, 256, 2)

        def _lstm(x, W_ih, W_hh, b_ih, b_hh):
            x_proj = jnp.einsum('btd,gd->btg', x, W_ih) + b_ih + b_hh
            h0 = jnp.zeros((x.shape[0], W_hh.shape[1]), x.dtype)
            c0 = jnp.zeros_like(h0)

            def step(carry, xp):
                h, c = carry
                gates = xp + h @ W_hh.T
                i, f, g, o = jnp.split(gates, 4, axis=-1)
                c = jax.nn.sigmoid(f) * c + jax.nn.sigmoid(i) * jnp.tanh(g)
                h = jax.nn.sigmoid(o) * jnp.tanh(c)
                return ((h, c), h)
            _, hs = jax.lax.scan(step, (h0, c0), jnp.swapaxes(x_proj, 0, 1))
            return jnp.swapaxes(hs, 0, 1)
        lstm_out = _lstm(x, W_ih, W_hh, b_ih, b_hh)
        logits = jnp.einsum('bth,lh->btl', lstm_out, W_lin) + b_lin
        g = jax.lax.stop_gradient(jnp.argmax(logits, axis=-1).astype(lstm_out.dtype))[..., None]
        w = g * lstm_out
        inc = jnp.cumsum(w, axis=1)
        prefix = inc - w
        suffix = inc[:, -1:, :] - inc
        return 2.0 * lstm_out + prefix * fw_att + suffix * bw_att
    edge_index = jnp.stack([src, dst])
    x = x + _L0_gnn_ref(_layernorm(x, axis=-1), edge_index, edge_weight, L0_gnn_W_weight, L0_gnn_W_bias)
    x = x + _L0_ffn_ref(_layernorm(x, axis=-1)[None], L0_ffn_W_ih, L0_ffn_W_hh, L0_ffn_b_ih, L0_ffn_b_hh, L0_ffn_W_lin, L0_ffn_b_lin, L0_ffn_fw_att, L0_ffn_bw_att)[0]
    return x

_drawn_inputs = setup_inputs


def setup_inputs(seed=0):
    import zlib

    import numpy as np

    out = dict(_drawn_inputs(seed))
    spreads = {'L0_ffn_fw_att': (0.0010000000474974513, 0.6),
     'L0_ffn_bw_att': (0.0010000000474974513, 0.6)}
    factors = {'L0_ffn_W_hh': 2.759, 'L0_ffn_b_ih': 3.451, 'L0_ffn_b_hh': 3.178, 'L0_ffn_W_lin': 6.603}
    for name, (base, spread) in spreads.items():
        noise = np.random.default_rng([zlib.crc32(name.encode()), seed]).standard_normal(out[name].shape)
        drawn = base * np.exp(spread * noise) if base else spread * noise
        out[name] = jnp.asarray(drawn.astype(out[name].dtype))
    for name, factor in factors.items():
        out[name] = (out[name] * factor).astype(out[name].dtype)
    return out
```

```python
from contextlib import ExitStack

import concourse.bass as bass
from concourse import mybir

N, D, E = 6250, 256, 100000
P = 128
G4 = 4 * D
EP, EC = 125, 800
NB = -(-N // P)
LASTB = N - (NB - 1) * P
TILES = (E + NB * (P - 1)) // P + 1
TU = 10
TILES = -(-TILES // TU) * TU
SEGS, SEGL = 125, 50
WARM = 74
SU = 16
CH = 160
NCH = EC // CH
XPR = WARM + N + WARM + SEGL
TOL = 2.0 ** -19
EPS = 1e-5
CLOSED = -1.0e4


def build(nc, A, out, slow_sweeps=SEGS - 1, tol=TOL):
    f32, i32, u8 = mybir.dt.float32, mybir.dt.int32, mybir.dt.uint8
    u32 = mybir.dt.uint32
    bf16 = mybir.dt.bfloat16
    ALU = mybir.AluOpType
    ACT = mybir.ActivationFunctionType
    AX = mybir.AxisListType
    ds = bass.ds
    RMAX = bass.bass_isa.ReduceOp.max

    sup_d = nc.dram_tensor("support_scratch", [NB * P, D], f32).ap()
    rec_d = nc.dram_tensor("record_scratch", [P * TILES, 3], f32).ap()
    xp_d = nc.dram_tensor("gate_input_scratch", [XPR, G4], f32).ap()
    x1_d = nc.dram_tensor("x1_scratch", [NB * P, D], f32).ap()

    with ExitStack() as ctx:
        def sb(name, shape, dt=f32):
            return ctx.enter_context(nc.sbuf_tensor(name, shape, dt))

        def pb(name, shape, dt=f32):
            return ctx.enter_context(nc.psum_tensor(name, shape, dt))

        def sem(name):
            return ctx.enter_context(nc.semaphore(name))

        big_a = sb("big_a", [P, NB + 1, D])
        big_b = sb("big_b", [P, NB + 1, D])
        big_c = sb("big_c", [P, NB + 1, D])
        consts = sb("consts_sb", [P, 5, P])
        ident, iota, before, shift, ones = (consts[:, i, :] for i in range(5))
        w_gnn = sb("w_gnn", [P, 2, D])
        b_gnn = sb("b_gnn", [P, D])
        w_ih = sb("w_ih", [P, 2, G4])
        b_ih = sb("b_ih_sb", [P, G4])
        b_hh = sb("b_hh_sb", [P, G4])
        w_lin = sb("w_lin", [P, 2, D])
        b_lin = sb("b_lin", [P, 2])
        fw = sb("fw", [P, D])
        bw = sb("bw", [P, D])
        records = sb("records", [P, TILES, 3])
        recs = records[:].rearrange("p t k -> p (t k)")[0:EP, 0:EC * 3].rearrange("p (c k) -> p c k", k=3)
        rec2 = records[:]
        posf = sb("posf", [EP, EC])
        cum = sb("cum", [EP, CH])
        cnt = sb("cnt", [EP, NB])
        pos0 = sb("pos0", [EP, NB])
        tot = sb("tot", [P, NB])
        tot_i = sb("tot_i", [P, NB], i32)
        tiles_f = sb("tiles_f", [P, NB])
        ends = sb("ends", [P, NB])
        ends_col = sb("ends_col", [NB, 1])
        table = sb("table", [1, TILES], i32)
        stg_i = sb("stg_i", [EP, 2, SU // 2], u32)
        stg_r = sb("stg_r", [EP, 2, SU // 2, 3])
        stg_g = sb("stg_g", [P, 2, TU // 2], u32)
        stg_w = sb("stg_w", [P, 2, TU // 2, 2])
        sums = sb("sums", [P, NB])
        var = sb("var", [P, NB])
        rstd = sb("rstd", [P, NB])
        tmp = sb("tmp", [P, NB])
        xn = sb("xn", [P, 2, D])
        xt = sb("xt", [P, 2, 2, P])
        pr = sb("pr", [P, 2, G4])
        gmax = sb("gmax", [P, 1])
        gall = sb("gall", [P, 1])
        flag = sb("flag", [1, 1], i32)

        spare = big_c[:].rearrange("p b f -> p (b f)")
        taken = {"rank": 0, "gather": 0, "lstm": 0}

        def part(stage, shape, dt=f32):
            size = 1
            for n in shape[1:]:
                size *= n
            at = taken[stage]
            taken[stage] += size
            view = spare[0:shape[0], at:at + size]
            if dt != f32:
                view = view.bitcast(dt)
            if len(shape) == 3:
                view = view.rearrange("p (a b) -> p a b", a=shape[1])
            return view

        src_sb = part("rank", [EP, EC], i32)
        dst_sb = part("rank", [EP, EC], i32)
        bk_i = part("rank", [EP, EC], i32)
        pos_i = part("rank", [EP, EC], i32)
        w_sb = part("rank", [EP, EC])
        bk = part("rank", [EP, EC])
        mask = part("rank", [EP, EC // 4]).bitcast(u8)
        bk_c = part("rank", [EP, CH])
        pos_c = part("rank", [EP, CH])
        mask_c = part("rank", [EP, CH // 4]).bitcast(u8)
        tile_iota = part("rank", [NB, TILES])
        tile_ge = part("rank", [NB, TILES])
        table_f = part("rank", [1, TILES])
        rows = part("gather", [P, TU, D])
        oneh = part("gather", [P, TU, P])
        w_hh = part("lstm", [P, 2, G4])
        xp = part("lstm", [SEGS, 2, G4])
        h_s = part("lstm", [SEGS, 2, D])
        c_s = part("lstm", [SEGS, 2, D])
        start = part("lstm", [SEGS, 2, D])
        gap = part("lstm", [P, 2, D])
        h_t = part("lstm", [P, 2, SEGS])
        act_g, act_i, act_f, act_o, act_c = (part("lstm", [SEGS, D]) for _ in range(5))
        late = records[:].rearrange("p t k -> p (t k)")
        run, diff, base, ig, fc = (late[0:SEGS, i * D:(i + 1) * D] for i in range(5))
        logit = late[0:SEGS, 5 * D:5 * D + 2 * SEGL].rearrange("p (a b) -> p a b", a=2)
        gate = late[0:SEGS, 6 * D:6 * D + SEGL]
        hs = big_a[0:SEGS, 0:SEGL, :]
        x1s = big_b[0:SEGS, 0:SEGL, :]
        wr = big_c[0:SEGS, 0:SEGL, :]

        bank = [pb(f"bank{i}", [P, 512]) for i in range(8)]

        load_w = sem("load_weights")
        load_r = sem("load_recurrent_weights")
        load_c = sem("load_constants")
        load_e = sem("load_edges")
        load_x = sem("load_x")
        zeroed = sem("zeroed")
        rec_zero = sem("records_zeroed")
        v = sem("vector_chain")
        counted = sem("edges_counted")
        prefixed = sem("counts_prefixed")
        ends_r = sem("bucket_ends_ready")
        ends_t = sem("ends_transposed")
        ge_done = sem("tile_compare_done")
        table_s = sem("tile_blocks_summed")
        table_r = sem("tile_table_ready")
        placed = sem("edges_placed")
        staged = sem("scatter_staged")
        scat = [sem(f"scattered{i}") for i in range(2)]
        go = sem("gpsimd_may_issue")
        dgo = sem("vector_may_loop")
        rec_l = sem("records_loaded")
        gst = sem("gather_staged")
        gat = [sem(f"gathered{i}") for i in range(TU)]
        oh_r = sem("onehot_ready")
        prod = sem("tile_product_done")
        added = sem("tile_added")
        var_r = sem("variance_ready")
        sq = sem("sqrt_done")
        cdone = sem("rows_centred")
        xn_r = sem("normalised_ready")
        xt_p = sem("transposed_in_psum")
        xt_r = sem("transposed_ready")
        pj = sem("projected")
        pr_r = sem("projection_copied")
        st0 = [sem(f"projection_stored{i}") for i in range(2)]
        xn_r2 = sem("normalised2_ready")
        xt_p2 = sem("transposed2_in_psum")
        xt_r2 = sem("transposed2_ready")
        pj2 = sem("projected2")
        pr_r2 = sem("projection2_copied")
        st2 = [sem(f"projection2_stored{i}") for i in range(2)]
        x1_r = sem("x1_ready")
        x1_st = sem("x1_stored")
        x1_ld = sem("x1_by_segment_loaded")
        pad_r = sem("pad_rows_ready")
        pad_s = sem("pad_rows_stored")
        xp_l = [sem(f"gate_input_loaded{i}") for i in range(2)]
        inj = sem("gate_input_in_psum")
        gi_r = sem("gates_gi_ready")
        f_r = sem("gate_f_ready")
        o_r = sem("gate_o_ready")
        a_gi = sem("act_gi_done")
        a_f = sem("act_f_done")
        a_o = sem("act_o_done")
        a_c = sem("tanh_c_done")
        s_m = sem("state_products_done")
        s_c = sem("c_ready")
        s_h = sem("h_ready")
        t_p = sem("h_transposed_in_psum")
        t_r = sem("h_transposed_ready")
        kept = sem("h_kept")
        shf = sem("state_shifted")
        gapd = sem("gap_measured")
        gapa = sem("gap_over_all")
        flg = sem("flag_ready")
        shs = sem("shift_copied")
        fin = sem("lstm_finished")
        segt = sem("segment_totals_ready")
        segp = sem("segment_prefix_done")
        res = sem("result_ready")
        out_s = sem("result_stored")

        block = ctx.enter_context(nc.Block())

        STEPS = WARM + SEGL
        TSLOW = STEPS + slow_sweeps * SEGL

        @block.sync
        def _(sp):
            sp.dma_start(src_sb, A["src"].rearrange("(p c) -> p c", p=EP)).then_inc(load_e, 16)
            sp.dma_start(dst_sb, A["dst"].rearrange("(p c) -> p c", p=EP)).then_inc(load_e, 16)
            sp.dma_start(w_sb, A["edge_weight"].rearrange("(p c) -> p c", p=EP)).then_inc(load_e, 16)
            sp.dma_start(consts[:], A["consts"].rearrange("k p f -> p k f")).then_inc(load_c, 16)
            sp.dma_start(tile_iota, A["tile_iota"].partition_broadcast(NB)).then_inc(load_c, 16)
            sp.wait_ge(zeroed, 1)
            sp.dma_start(big_a[:, 0:NB - 1, :], A["x"][0:(NB - 1) * P, :].rearrange("(b p) f -> p b f", p=P)
                         ).then_inc(load_x, 16)
            sp.dma_start(big_a[0:LASTB, NB - 1, :], A["x"][(NB - 1) * P:N, :]).then_inc(load_x, 16)
            sp.wait_ge(zeroed, 2)
            sp.dma_start(rec_d.rearrange("(p t) k -> p (t k)", p=P),
                         rec2.rearrange("p t k -> p (t k)")).then_inc(rec_zero, 16)
            for k, (name, tile) in enumerate([("w_gnn", w_gnn), ("w_ih", w_ih)]):
                sp.dma_start(tile[:], A[name].rearrange("(k p) f -> p k f", p=P)).then_inc(load_w, 16)
            sp.dma_start(b_gnn[:], A["b_gnn"].partition_broadcast(P)).then_inc(load_w, 16)
            sp.dma_start(b_ih[:], A["b_ih"].partition_broadcast(P)).then_inc(load_w, 16)
            sp.dma_start(b_hh[:], A["b_hh"].partition_broadcast(P)).then_inc(load_w, 16)
            for l in range(2):
                sp.dma_start(w_lin[:, l, :], A["w_lin"][l, :].partition_broadcast(P)).then_inc(load_w, 16)
            sp.dma_start(b_lin[:], A["b_lin"].partition_broadcast(P)).then_inc(load_w, 16)
            sp.dma_start(fw[:], A["fw"].partition_broadcast(P)).then_inc(load_w, 16)
            sp.dma_start(bw[:], A["bw"].partition_broadcast(P)).then_inc(load_w, 16)

            def store_support(t, q, nth):
                first = sp.snap(t * P) if not isinstance(t, int) else t * P
                sp.wait_ge(pr_r, t + 1)
                sp.dma_start(sup_d[ds(first, P), :], pr[:, q, 0:D]).then_inc(st0[q], 16)

            with sp.Fori(0, NB // 2) as it:
                store_support(it * 2, 0, it)
                store_support(it * 2 + 1, 1, it)
            store_support(NB - 1, 0, NB // 2)

            for q in range(2):
                sp.wait_ge(scat[q], 16 * EC // 2)
            sp.dma_start(rec2.rearrange("p t k -> p (t k)"),
                         rec_d.rearrange("(p t) k -> p (t k)", p=P)).then_inc(rec_l, 16)

            sp.wait_ge(pad_r, 1)
            sp.dma_start(xp_d[0:WARM, :], pr[0:WARM, 0, :]).then_inc(pad_s, 16)
            sp.wait_ge(x1_r, 1)
            sp.dma_start(x1_d.rearrange("(b p) f -> p b f", p=P), big_b[:, 0:NB, :]).then_inc(x1_st, 16)

            def store_gate_input(t, q):
                first = sp.snap(t * P + WARM) if not isinstance(t, int) else t * P + WARM
                sp.wait_ge(pr_r2, t + 1)
                sp.dma_start(xp_d[ds(first, P), :], pr[:, q, :]).then_inc(st2[q], 16)

            sp.wait_ge(pad_s, 16)
            with sp.Fori(0, NB // 2) as it:
                store_gate_input(it * 2, 0)
                store_gate_input(it * 2 + 1, 1)
            store_gate_input(NB - 1, 0)
            sp.wait_ge(pr_r2, NB)
            sp.dma_start(w_hh, A["w_hh"].rearrange("(k p) f -> p k f", p=P)).then_inc(load_r, 16)
            sp.wait_ge(st2[0], 16 * (NB // 2 + 1))
            sp.wait_ge(st2[1], 16 * (NB // 2))
            sp.wait_ge(x1_st, 16)
            sp.dma_start(x1s, x1_d[0:N, :].rearrange("(k l) f -> k l f", l=SEGL)).then_inc(x1_ld, 16)

            def load_gate_input(u, t, q, first=False):
                row = t if isinstance(t, int) else sp.snap(t)
                if not first:
                    sp.wait_ge(inj, u - 1)
                sp.dma_start(xp[:, q, :], xp_d[ds(row, SEGS, step=SEGL), :]).then_inc(xp_l[q], 16)

            load_gate_input(0, 0, 0, True)
            load_gate_input(1, 1, 1, True)
            with sp.Fori(1, STEPS // 2) as it:
                load_gate_input(it * 2, it * 2, 0)
                load_gate_input(it * 2 + 1, it * 2 + 1, 1)
            sp.wait_ge(flg, 1)
            ok = sp.value_load(flag[0:1, 0:1], min_val=0, max_val=1)
            with sp.If(ok == 0):
                with sp.Fori(0, slow_sweeps) as sweep:
                    with sp.Fori(0, SEGL // 2) as it:
                        for q in range(2):
                            load_gate_input(sweep * SEGL + it * 2 + (STEPS + q), it * 2 + (WARM + q), q)

            sp.wait_ge(res, 1)
            sp.dma_start(out.rearrange("(k l) f -> k l f", l=SEGL), wr).then_inc(out_s, 16)
            sp.wait_ge(out_s, 16)

        @block.gpsimd
        def _(pool):
            nc.gpsimd.memset(big_a[:, NB - 1, :], 0.0).then_inc(zeroed, 1)
            nc.gpsimd.memset(rec2, 0.0).then_inc(zeroed, 1)
            nc.gpsimd.memset(big_b[:], 0.0).then_inc(zeroed, 1)
            pool.wait_ge(rec_zero, 16)
            HU = SU // 2

            with pool.Fori(0, EC // SU) as it:
                for q in range(2):
                    pool.wait_ge(staged, it * 2 + (q + 1))
                    pool.sem_inc(go, 1)
                    for j in range(HU):
                        pool.indirect_dma_start(
                            out=rec_d, out_offset=bass.IndirectOffsetOnAxis(ap=stg_i[:, q, j:j + 1], axis=0),
                            in_=stg_r[:, q, j, :], in_offset=None).then_inc(scat[q], 16)

            GU = TU // 2
            for q in range(2):
                pool.wait_ge(st0[q], 16 * (NB // 2 + 1 - q))

            def gather(it):
                for q in range(2):
                    pool.wait_ge(gst, it * 2 + (q + 1))
                    pool.sem_inc(go, 1)
                    for j in range(GU):
                        s = q * GU + j
                        pool.indirect_dma_start(
                            out=rows[:, s, :], out_offset=None, in_=sup_d,
                            in_offset=bass.IndirectOffsetOnAxis(ap=stg_g[:, q, j:j + 1], axis=0)
                        ).then_inc(gat[s], 16)

            with pool.Fori(0, TILES // TU) as it:
                gather(it)

            pool.wait_ge(s_h, WARM)
            nc.gpsimd.tensor_copy(start[:, 0, :], h_s[:, 1, :])
            nc.gpsimd.tensor_copy(start[:, 1, :], c_s[:, 1, :]).then_inc(kept, 1)

            def keep(u, j, q):
                pool.wait_ge(s_h, u + 1)
                nc.gpsimd.tensor_copy(hs[:, ds(j, 1), :], h_s[:, q:q + 1, :]).then_inc(kept, 1)

            with pool.Fori(0, SEGL // 2) as it:
                for q in range(2):
                    keep(it * 2 + (WARM + q), it * 2 + q, q)
            pool.wait_ge(kept, SEGL + 1)
            pool.wait_ge(gapd, 1)
            nc.gpsimd.partition_all_reduce(gall[:], gmax[:], P, RMAX).then_inc(gapa, 1)
            pool.wait_ge(flg, 1)
            ok = pool.value_load(flag[0:1, 0:1], min_val=0, max_val=1)
            with pool.If(ok == 0):
                with pool.Fori(0, slow_sweeps) as sweep:
                    with pool.Fori(0, SEGL // 2) as it:
                        for q in range(2):
                            keep(sweep * SEGL + it * 2 + (STEPS + q), it * 2 + q, q)
                pool.wait_ge(kept, SEGL * (slow_sweeps + 1) + 1)
            pool.sem_inc(fin, 1)

        @block.scalar
        def _(act):
            HU = SU // 2
            GU = TU // 2

            def stage_scatter(it, q, first=False):
                if not first:
                    act.wait_ge(scat[q], it * (16 * HU))
                nc.scalar.copy(stg_i[:, q, :], posf[:, ds(it * SU + q * HU, HU)])
                nc.scalar.copy(stg_r[:, q, :, :], recs[:, ds(it * SU + q * HU, HU), :]).then_inc(staged, 1)

            def sqrt_var():
                act.wait_ge(var_r, 1)
                nc.scalar.activation(tmp[:], var[:], ACT.Sqrt).then_inc(sq, 1)

            def copy_transposed(t, q, ready, used, out_ready, first=False):
                act.wait_ge(ready, t + 1)
                if not first:
                    act.wait_ge(used, t - 1)
                nc.scalar.copy(xt[:, q, :, :], bank[q][:, 0:2 * P].rearrange("p (k n) -> p k n", k=2)
                               ).then_inc(out_ready, 1)

            act.wait_ge(placed, 1)
            stage_scatter(0, 0, True)
            stage_scatter(0, 1, True)
            sqrt_var()
            copy_transposed(0, 0, xt_p, pj, xt_r, True)
            stage_scatter(1, 0)
            copy_transposed(1, 1, xt_p, pj, xt_r, True)
            stage_scatter(1, 1)
            with act.Fori(2, NB // 2 + 1) as it:
                copy_transposed(it * 2 - 2, 0, xt_p, pj, xt_r)
                stage_scatter(it, 0)
                copy_transposed(it * 2 - 1, 1, xt_p, pj, xt_r)
                stage_scatter(it, 1)
            copy_transposed(NB - 1, 0, xt_p, pj, xt_r)
            with act.Fori(NB // 2 + 1, EC // SU) as it:
                stage_scatter(it, 0)
                stage_scatter(it, 1)

            def stage_gather(it, q, first=False):
                if not first:
                    act.wait_ge(prod, it * TU + (q * GU + GU - TU))
                src = rec2[:, ds(it * TU + q * GU, GU), :]
                nc.scalar.copy(stg_g[:, q, :], src[:, :, 0])
                nc.scalar.copy(stg_w[:, q, :, :], src[:, :, 1:3]).then_inc(gst, 1)

            act.wait_ge(rec_l, 16)
            stage_gather(0, 0, True)
            stage_gather(0, 1, True)
            with act.Fori(1, TILES // TU) as it:
                stage_gather(it, 0)
                stage_gather(it, 1)

            act.wait_ge(var_r, 2)
            nc.scalar.activation(tmp[:], var[:], ACT.Sqrt).then_inc(sq, 1)
            copy_transposed(0, 0, xt_p2, pj2, xt_r2, True)
            copy_transposed(1, 1, xt_p2, pj2, xt_r2, True)
            with act.Fori(1, NB // 2) as it:
                copy_transposed(it * 2, 0, xt_p2, pj2, xt_r2)
                copy_transposed(it * 2 + 1, 1, xt_p2, pj2, xt_r2)
            copy_transposed(NB - 1, 0, xt_p2, pj2, xt_r2)

            def step(u, q):
                act.wait_ge(gi_r, u + 1)
                nc.scalar.activation(act_g, bank[3 * q][0:SEGS, 0:D], ACT.Tanh)
                nc.scalar.activation(act_i, bank[3 * q][0:SEGS, D:2 * D], ACT.Sigmoid).then_inc(a_gi, 1)
                act.wait_ge(f_r, u + 1)
                nc.scalar.activation(act_f, bank[3 * q + 1][0:SEGS, 0:D], ACT.Sigmoid).then_inc(a_f, 1)
                act.wait_ge(o_r, u + 1)
                nc.scalar.activation(act_o, bank[3 * q + 2][0:SEGS, 0:D], ACT.Sigmoid).then_inc(a_o, 1)
                act.wait_ge(s_c, u + 1)
                nc.scalar.activation(act_c, c_s[:, q, :], ACT.Tanh).then_inc(a_c, 1)

            with act.Fori(0, STEPS // 2) as it:
                step(it * 2, 0)
                step(it * 2 + 1, 1)
            act.wait_ge(flg, 1)
            ok = act.value_load(flag[0:1, 0:1], min_val=0, max_val=1)
            with act.If(ok == 0):
                with act.Fori(0, slow_sweeps) as sweep:
                    with act.Fori(0, SEGL // 2) as it:
                        for q in range(2):
                            step(sweep * SEGL + it * 2 + (STEPS + q), q)

        @block.vector
        def _(dve):
            count = [0]

            def link(ins):
                count[0] += 1
                ins.then_inc(v, 1)
                dve.wait_ge(v, count[0])

            V = nc.vector
            dve.wait_ge(load_e, 48)
            V.tensor_scalar(bk_i, src_sb, 7, None, ALU.arith_shift_right)
            link(V.tensor_scalar(pos_i, src_sb, P - 1, None, ALU.bitwise_and))
            dve.wait_ge(rec_zero, 16)
            V.tensor_copy(recs[:, :, 2], pos_i)
            V.tensor_copy(recs[:, :, 1], w_sb)
            V.tensor_copy(recs[:, :, 0], dst_sb)
            link(V.tensor_copy(bk, bk_i))
            dve.wait_ge(load_c, 32)
            with dve.Fori(0, NB) as b:
                V.tensor_scalar(mask, bk, iota[0:EP, ds(b, 1)], None, ALU.is_equal).then_inc(v, 1)
                dve.wait_ge(v, b * 2 + (count[0] + 1))
                V.tensor_reduce(cnt[:, ds(b, 1)], mask, AX.X, ALU.add).then_inc(v, 1)
                dve.wait_ge(v, b * 2 + (count[0] + 2))
            count[0] += 2 * NB
            V.memset(pos_c, 0.0).then_inc(counted, 1)
            dve.wait_ge(prefixed, 1)
            link(V.tensor_copy(tot[:], bank[0][:, 0:NB]))
            link(V.tensor_scalar(tot_i[:], tot[:], float(P - 1), None, ALU.add))
            link(V.tensor_scalar(tot_i[:], tot_i[:], 7, None, ALU.arith_shift_right))
            link(V.tensor_copy(tiles_f[:], tot_i[:]))
            link(V.tensor_tensor_scan(ends[:], tiles_f[:], tiles_f[:], 0.0, ALU.add, ALU.bypass))
            link(V.tensor_tensor(tmp[:], ends[:], tiles_f[:], ALU.subtract))
            link(V.tensor_scalar(tmp[:], tmp[:], float(P), -1.0, ALU.mult, ALU.add))
            V.tensor_tensor(pos0[:], tmp[0:EP, :], bank[1][0:EP, 0:NB], ALU.add).then_inc(ends_r, 1)
            dve.wait_ge(ends_r, 1)

            each = 4 * NB + 2
            with dve.Fori(0, NCH) as c:
                V.tensor_scalar(bk_c, bk[:, ds(c * CH, CH)], 0.0, None, ALU.add).then_inc(v, 1)
                dve.wait_ge(v, c * each + (count[0] + 1))
                dve.sem_inc(dgo, 1)
                with dve.Fori(0, NB) as b:
                    n = c * each + b * 4 + (count[0] + 1)
                    V.tensor_scalar(mask_c, bk_c, iota[0:EP, ds(b, 1)], None, ALU.is_equal).then_inc(v, 1)
                    dve.wait_ge(v, n + 1)
                    V.tensor_tensor_scan(cum[:], mask_c, mask_c, pos0[:, ds(b, 1)], ALU.add, ALU.bypass).then_inc(v, 1)
                    dve.wait_ge(v, n + 2)
                    V.tensor_scalar(pos0[:, ds(b, 1)], cum[:, CH - 1:CH], 0.0, None, ALU.add).then_inc(v, 1)
                    V.copy_predicated(pos_c, mask_c, cum[:]).then_inc(v, 1)
                    dve.wait_ge(v, n + 4)
                V.tensor_scalar(posf[:, ds(c * CH, CH)], pos_c, 0.0, None, ALU.add).then_inc(v, 1)
                dve.wait_ge(v, c * each + (count[0] + each))
            count[0] += each * NCH
            link(V.tensor_copy(pos_i, posf[:]))
            V.tensor_scalar(bk_i, pos_i, 7, None, ALU.arith_shift_right)
            link(V.tensor_scalar(pos_i, pos_i, P - 1, None, ALU.bitwise_and))
            link(V.tensor_copy(bk, bk_i))
            V.scalar_tensor_tensor(posf[:], pos_i, float(TILES), bk, ALU.mult, ALU.add).then_inc(placed, 1)

            dve.wait_ge(ends_t, 1)
            link(V.tensor_copy(ends_col[:], bank[2][0:NB, 0:1]))
            V.tensor_scalar(tile_ge, tile_iota, ends_col[:, 0:1], None, ALU.is_ge).then_inc(ge_done, 1)
            dve.wait_ge(table_s, 1)
            V.tensor_scalar(table_f[0:1, 0:512], bank[3][0:1, 0:512], float(NB - 1), float(D), ALU.min, ALU.mult)
            link(V.tensor_scalar(table_f[0:1, 512:TILES], bank[4][0:1, 0:TILES - 512], float(NB - 1), float(D),
                                 ALU.min, ALU.mult))
            link(V.tensor_copy(table[:], table_f))

            def norm(rowsin, nth):
                link(V.tensor_reduce(sums[:], rowsin, AX.X, ALU.add))
                link(V.tensor_scalar(sums[:], sums[:], 1.0 / D, None, ALU.mult))
                link(V.tensor_tensor(big_c[:, 0:NB, :], rowsin,
                                     sums[:].rearrange("p (b o) -> p b o", o=1).broadcast_to([P, NB, D]), ALU.subtract))
                squares = pr[:].rearrange("p a (b f) -> p (a b) f", f=D)
                with dve.Fori(0, NB // 8) as b:
                    n = b * 2 + count[0]
                    part_c = big_c[:, ds(b * 8, 8), :]
                    V.tensor_tensor(squares, part_c, part_c, ALU.mult).then_inc(v, 1)
                    dve.wait_ge(v, n + 1)
                    V.tensor_reduce(sums[:, ds(b * 8, 8)], squares, AX.X, ALU.add).then_inc(v, 1)
                    dve.wait_ge(v, n + 2)
                count[0] += NB // 8 * 2
                link(V.tensor_tensor(squares[:, 0, :], big_c[:, NB - 1, :], big_c[:, NB - 1, :], ALU.mult))
                link(V.tensor_reduce(sums[:, NB - 1:NB], squares[:, 0, :], AX.X, ALU.add))
                V.tensor_scalar(var[:], sums[:], 1.0 / D, EPS, ALU.mult, ALU.add).then_inc(var_r, 1)
                dve.wait_ge(sq, nth)
                link(V.reciprocal(rstd[:], tmp[:]))
                link(V.tensor_tensor(tmp[:], rstd[:], rstd[:], ALU.mult))
                link(V.tensor_tensor(tmp[:], tmp[:], var[:], ALU.mult))
                link(V.tensor_scalar(tmp[:], tmp[:], -0.5, 1.5, ALU.mult, ALU.add))
                link(V.tensor_tensor(rstd[:], rstd[:], tmp[:], ALU.mult))

            def normalise(t, q, ready, free, first=False):
                if not first:
                    dve.wait_ge(free, t - 1)
                V.tensor_scalar(xn[:, q:q + 1, :], big_c[:, ds(t, 1), :], rstd[:, ds(t, 1)], None,
                                ALU.mult).then_inc(ready, 1)

            def evacuate_support(t, q, first=False):
                dve.wait_ge(pj, t + 1)
                if not first:
                    dve.wait_ge(st0[q], t * 8 - q * 8)
                V.tensor_tensor(pr[:, q, 0:D], bank[2 + q][:, 0:D], b_gnn[:], ALU.add).then_inc(pr_r, 1)

            dve.wait_ge(load_x, 32)
            dve.wait_ge(zeroed, 1)
            norm(big_a[:, 0:NB, :], 1)
            dve.wait_ge(load_w, 16 * 10)
            V.tensor_tensor(b_ih[:], b_ih[:], b_hh[:], ALU.add)
            normalise(0, 0, xn_r, xt_p, True)
            normalise(1, 1, xn_r, xt_p, True)
            evacuate_support(0, 0, True)
            normalise(2, 0, xn_r, xt_p)
            evacuate_support(1, 1, True)
            normalise(3, 1, xn_r, xt_p)
            with dve.Fori(1, NB // 2 - 1) as it:
                evacuate_support(it * 2, 0)
                normalise(it * 2 + 2, 0, xn_r, xt_p)
                evacuate_support(it * 2 + 1, 1)
                normalise(it * 2 + 3, 1, xn_r, xt_p)
            evacuate_support(NB - 3, 0)
            normalise(NB - 1, 0, xn_r, xt_p)
            evacuate_support(NB - 2, 1)
            evacuate_support(NB - 1, 0)
            dve.wait_ge(st0[0], 16 * (NB // 2 + 1))
            dve.wait_ge(st0[1], 16 * (NB // 2))
            link(V.memset(pr[:], 0.0))
            V.memset(pr[0:WARM, 0, D:2 * D], CLOSED)
            V.memset(pr[0:WARM, 0, 3 * D:4 * D], CLOSED).then_inc(pad_r, 1)

            GU = TU // 2
            regs = [dve.alloc_register(f"tile_block{s}") for s in range(TU)]
            acc = big_b[:].rearrange("p b f -> p (b f)")

            def onehots(it, q):
                dve.wait_ge(gst, it * 2 + q + 1)
                for j in range(GU):
                    s = q * GU + j
                    V.tensor_scalar(oneh[:, s, :], iota[:], stg_w[:, q, j, 1:2], stg_w[:, q, j, 0:1],
                                    ALU.is_equal, ALU.mult).then_inc(oh_r, 1)

            def add_tiles(it, q, vals):
                for j in range(GU):
                    s = q * GU + j
                    dve.wait_ge(prod, it * TU + (s + 1))
                    at = acc[:, ds(vals[s], D)]
                    V.tensor_tensor(at, at, bank[s % 2][:, 0:D], ALU.add).then_inc(added, 1)
                    dve.wait_ge(added, it * TU + (s + 1))

            dve.wait_ge(zeroed, 3)
            onehots(0, 0)
            def blocks(it):
                dve.reg_load(regs, table[0:1, ds(it * TU, TU)])
                return [dve.snap(r, min_val=0, max_val=(NB - 1) * D) for r in regs]
            with dve.Fori(0, TILES // TU - 1) as it:
                vals = blocks(it)
                onehots(it, 1)
                add_tiles(it, 0, vals)
                onehots(it + 1, 0)
                add_tiles(it, 1, vals)
            last = TILES // TU - 1
            vals = blocks(last)
            onehots(last, 1)
            add_tiles(last, 0, vals)
            add_tiles(last, 1, vals)

            dve.wait_ge(pad_s, 16)
            V.tensor_tensor(big_b[:, 0:NB, :], big_b[:, 0:NB, :], big_a[:, 0:NB, :], ALU.add).then_inc(x1_r, 1)
            dve.wait_ge(x1_r, 1)
            norm(big_b[:, 0:NB, :], 2)

            def evacuate_gates(t, q, first=False):
                dve.wait_ge(pj2, t + 1)
                if not first:
                    dve.wait_ge(st2[q], t * 8 - q * 8)
                for c in range(2):
                    last = V.tensor_tensor(pr[:, q, c * 512:c * 512 + 512], bank[2 + 2 * q + c][:],
                                           b_ih[:, c * 512:c * 512 + 512], ALU.add)
                last.then_inc(pr_r2, 1)

            dve.wait_ge(pad_s, 16)
            normalise(0, 0, xn_r2, xt_p2, True)
            normalise(1, 1, xn_r2, xt_p2, True)
            evacuate_gates(0, 0, True)
            normalise(2, 0, xn_r2, xt_p2)
            evacuate_gates(1, 1, True)
            normalise(3, 1, xn_r2, xt_p2)
            with dve.Fori(1, NB // 2 - 1) as it:
                evacuate_gates(it * 2, 0)
                normalise(it * 2 + 2, 0, xn_r2, xt_p2)
                evacuate_gates(it * 2 + 1, 1)
                normalise(it * 2 + 3, 1, xn_r2, xt_p2)
            evacuate_gates(NB - 3, 0)
            normalise(NB - 1, 0, xn_r2, xt_p2)
            evacuate_gates(NB - 2, 1)
            evacuate_gates(NB - 1, 0)

            V.memset(gap, 0.0)
            V.memset(c_s, 0.0).then_inc(s_m, 1)
            V.memset(h_t, 0.0).then_inc(t_r, 1)
            dve.wait_ge(s_m, 1)

            def step(u, q, extra, own=None):
                dve.wait_ge(a_gi, u + 1)
                V.tensor_tensor(ig, act_g, act_i, ALU.mult).then_inc(s_m, 1)
                dve.wait_ge(a_f, u + 1)
                V.tensor_tensor(fc, act_f, c_s[:, 1 - q, :], ALU.mult).then_inc(s_m, 1)
                if own is not None:
                    dve.wait_ge(kept, own)
                dve.wait_ge(s_m, u * 2 + 3)
                V.tensor_tensor(c_s[:, q, :], ig, fc, ALU.add).then_inc(s_c, 1)
                dve.wait_ge(a_c, u + 1)
                V.tensor_tensor(h_s[:, q, :], act_o, act_c, ALU.mult).then_inc(s_h, 1)
                copy_h(u + extra)

            def copy_h(n):
                dve.wait_ge(t_p, n + 1)
                V.tensor_copy(h_t, bank[6][:, 0:2 * P].rearrange("p (k n) -> p k n", k=2)[:, :, 0:SEGS]
                              ).then_inc(t_r, 1)

            with dve.Fori(0, WARM // 2) as it:
                step(it * 2, 0, 0)
                step(it * 2 + 1, 1, 0)
            with dve.Fori(0, SEGL // 2) as it:
                for q in range(2):
                    step(it * 2 + (WARM + q), q, 0, it * 2 + 1)

            dve.wait_ge(shf, 1)
            dve.wait_ge(kept, 1)
            for k in range(2):
                ins = V.tensor_tensor(gap[0:SEGS, k, :], bank[7][0:SEGS, k * D:(k + 1) * D], start[:, k, :],
                                      ALU.subtract)
            link(ins)
            V.tensor_reduce(gmax[:], gap, AX.XY, ALU.max, apply_absolute_value=True).then_inc(gapd, 1)
            dve.wait_ge(gapa, 1)
            V.tensor_scalar(flag[:], gall[0:1, :], tol, None, ALU.is_le).then_inc(flg, 1)
            dve.wait_ge(flg, 1)
            ok = dve.value_load(flag[0:1, 0:1], min_val=0, max_val=1)
            with dve.If(ok == 0):
                with dve.Fori(0, slow_sweeps) as sweep:
                    dve.wait_ge(shf, sweep + 1)
                    dve.wait_ge(kept, sweep * SEGL + (SEGL + 1))
                    V.tensor_copy(h_s[:, 1, :], bank[7][0:SEGS, 0:D])
                    V.tensor_copy(c_s[:, 1, :], bank[7][0:SEGS, D:2 * D]).then_inc(shs, 1)
                    dve.wait_ge(shs, sweep + 1)
                    copy_h(sweep * (SEGL + 1) + STEPS)
                    dve.sem_inc(dgo, 1)
                    with dve.Fori(0, SEGL // 2) as it:
                        for q in range(2):
                            step(sweep * SEGL + it * 2 + (STEPS + q), q, sweep + 1,
                                 sweep * SEGL + it * 2 + (SEGL + q))

                dve.wait_ge(shf, slow_sweeps + 1)
                dve.wait_ge(t_r, STEPS + slow_sweeps * (SEGL + 1) + 1)
                dve.sem_inc(dgo, 1)

            dve.wait_ge(fin, 1)
            for l in range(2):
                link(V.tensor_tensor(wr, hs, w_lin[0:SEGS, l:l + 1, :].broadcast_to([SEGS, SEGL, D]), ALU.mult))
                link(V.tensor_reduce(logit[:, l, :], wr, AX.X, ALU.add))
            link(V.tensor_scalar(logit[:, 0, :], logit[:, 0, :], b_lin[0:SEGS, 0:1], None, ALU.add))
            link(V.scalar_tensor_tensor(gate, logit[:, 1, :], b_lin[0:SEGS, 1:2], logit[:, 0, :],
                                        ALU.add, ALU.is_gt))
            link(V.tensor_tensor(wr, hs, gate.rearrange("k (l o) -> k l o", o=1).broadcast_to([SEGS, SEGL, D]),
                                 ALU.mult))
            V.tensor_reduce(run, wr.rearrange("k l f -> k f l"), AX.X, ALU.add).then_inc(segt, 1)
            V.tensor_tensor(diff, fw[0:SEGS, :], bw[0:SEGS, :], ALU.subtract)
            dve.wait_ge(segp, 1)
            link(V.tensor_tensor(base, bank[6][0:SEGS, D:2 * D], bw[0:SEGS, :], ALU.mult))
            link(V.tensor_tensor(run, bank[6][0:SEGS, 0:D], diff, ALU.mult))
            link(V.tensor_tensor(run, run, base, ALU.add))
            dve.wait_ge(x1_ld, 16)
            with dve.Fori(0, SEGL) as j:
                n = j * 4 + count[0]
                V.tensor_tensor(ig, wr[:, ds(j, 1), :].rearrange("k l f -> k (l f)"), diff, ALU.mult).then_inc(v, 1)
                V.scalar_tensor_tensor(fc, hs[:, ds(j, 1), :].rearrange("k l f -> k (l f)"), 2.0,
                                       x1s[:, ds(j, 1), :].rearrange("k l f -> k (l f)"), ALU.mult, ALU.add)
                V.tensor_tensor(base, wr[:, ds(j, 1), :].rearrange("k l f -> k (l f)"), fw[0:SEGS, :], ALU.mult
                                ).then_inc(v, 1)
                dve.wait_ge(v, n + 2)
                V.tensor_tensor(run, run, ig, ALU.add)
                V.tensor_tensor(fc, fc, base, ALU.subtract).then_inc(v, 1)
                dve.wait_ge(v, n + 3)
                V.tensor_tensor(wr[:, ds(j, 1), :].rearrange("k l f -> k (l f)"), fc, run, ALU.add).then_inc(v, 1)
                dve.wait_ge(v, n + 4)
            count[0] += 4 * SEGL
            V.memset(run[0:1, 0:1], 0.0).then_inc(res, 1)

        @block.tensor
        def _(pe):
            mm = nc.tensor.matmul
            pe.wait_ge(load_c, 32)
            pe.wait_ge(counted, 1)
            mm(bank[1][0:EP, 0:NB], before[0:EP, 0:EP], cnt[:], start=True, stop=True)
            mm(bank[0][:, 0:NB], ones[0:EP, :], cnt[:], start=True, stop=True).then_inc(prefixed, 1)
            pe.wait_ge(ends_r, 1)
            mm(bank[2][0:NB, 0:1], ends[0:1, :], ones[0:1, 0:1], start=True, stop=True).then_inc(ends_t, 1)
            pe.wait_ge(ge_done, 1)
            mm(bank[3][0:1, 0:512], ones[0:NB, 0:1], tile_ge[:, 0:512], start=True, stop=True)
            mm(bank[4][0:1, 0:TILES - 512], ones[0:NB, 0:1], tile_ge[:, 512:TILES], start=True, stop=True
               ).then_inc(table_s, 1)

            def transpose_rows(t, q, ready, copied, done, first=False):
                pe.wait_ge(ready, t + 1)
                if not first:
                    pe.wait_ge(copied, t - 1)
                for k in range(2):
                    ins = nc.tensor.transpose(bank[q][:, k * P:(k + 1) * P], xn[:, q, k * P:(k + 1) * P], ident[:])
                ins.then_inc(done, 1)

            def project_support(t, q, first=False):
                pe.wait_ge(xt_r, t + 1)
                if not first:
                    pe.wait_ge(pr_r, t - 1)
                for k in range(2):
                    ins = mm(bank[2 + q][:, 0:D], xt[:, q, k, :], w_gnn[:, k, :], start=k == 0, stop=k == 1)
                ins.then_inc(pj, 1)

            def project_gates(t, q, first=False):
                pe.wait_ge(xt_r2, t + 1)
                if not first:
                    pe.wait_ge(pr_r2, t - 1)
                for c in range(2):
                    for k in range(2):
                        ins = mm(bank[2 + 2 * q + c][:], xt[:, q, k, :], w_ih[:, k, c * 512:(c + 1) * 512],
                                 start=k == 0, stop=k == 1)
                ins.then_inc(pj2, 1)

            def all_blocks(project, ready, copied, done):
                transpose_rows(0, 0, ready, copied, done, True)
                transpose_rows(1, 1, ready, copied, done, True)
                project(0, 0, True)
                transpose_rows(2, 0, ready, copied, done)
                project(1, 1, True)
                transpose_rows(3, 1, ready, copied, done)
                with pe.Fori(1, NB // 2 - 1) as it:
                    project(it * 2, 0)
                    transpose_rows(it * 2 + 2, 0, ready, copied, done)
                    project(it * 2 + 1, 1)
                    transpose_rows(it * 2 + 3, 1, ready, copied, done)
                project(NB - 3, 0)
                transpose_rows(NB - 1, 0, ready, copied, done)
                project(NB - 2, 1)
                project(NB - 1, 0)

            pe.wait_ge(load_w, 16 * 10)
            all_blocks(project_support, xn_r, xt_r, xt_p)

            def tile_products(it, first=False):
                for s in range(TU):
                    pe.wait_ge(oh_r, it * TU + (s + 1))
                    pe.wait_ge(gat[s], it * 16 + 16)
                    if not (first and s < 2):
                        pe.wait_ge(added, it * TU + (s - 1))
                    mm(bank[s % 2][:, 0:D], oneh[:, s, :], rows[:, s, :], start=True, stop=True).then_inc(prod, 1)

            tile_products(0, True)
            with pe.Fori(1, TILES // TU) as it:
                tile_products(it)

            all_blocks(project_gates, xn_r2, xt_r2, xt_p2)

            PARTS = ((0, 0, 2 * D, gi_r), (1, 2 * D, D, f_r), (2, 3 * D, D, o_r))

            def inject(u, nth, q, first=False):
                pe.wait_ge(xp_l[q], nth * 16 + 16)
                if not first:
                    pe.wait_ge(a_o, u - 1)
                for c, at, width, _ in PARTS:
                    ins = mm(bank[3 * q + c][0:SEGS, 0:width], ident[0:SEGS, 0:SEGS], xp[:, q, at:at + width],
                             start=True, stop=False)
                ins.then_inc(inj, 1)

            def recur(u, q, extra):
                pe.wait_ge(t_r, u + extra + 1)
                for c, at, width, ready in PARTS:
                    for k in range(2):
                        ins = mm(bank[3 * q + c][0:SEGS, 0:width], h_t[:, k, :], w_hh[:, k, at:at + width],
                                 start=False, stop=k == 1)
                    ins.then_inc(ready, 1)

            def transpose_h(q):
                for k in range(2):
                    ins = nc.tensor.transpose(bank[6][:, k * P:k * P + SEGS], h_s[:, q, k * P:(k + 1) * P],
                                              ident[0:SEGS, 0:SEGS])
                ins.then_inc(t_p, 1)

            def shift_state():
                for k, state in enumerate((h_s, c_s)):
                    ins = mm(bank[7][0:SEGS, k * D:(k + 1) * D], shift[0:SEGS, 0:SEGS], state[:, 1, :],
                             start=True, stop=True)
                ins.then_inc(shf, 1)

            def pair(u, nth, extra, last=False):
                for q in range(2):
                    recur(u + q, q, extra)
                    if not (last and q):
                        inject(u + (q + 1), nth + q, 1 - q)
                    pe.wait_ge(s_h, u + (q + 1))
                    transpose_h(q)

            pe.wait_ge(pr_r2, NB)
            pe.wait_ge(load_r, 16)
            inject(0, 0, 0, True)
            recur(0, 0, 0)
            inject(1, 0, 1, True)
            pe.wait_ge(s_h, 1)
            transpose_h(0)
            recur(1, 1, 0)
            inject(2, 1, 0)
            pe.wait_ge(s_h, 2)
            transpose_h(1)
            with pe.Fori(1, STEPS // 2 - 1) as it:
                pair(it * 2, it, 0)
            pair(STEPS - 2, STEPS // 2 - 1, 0, True)
            shift_state()
            pe.wait_ge(flg, 1)
            ok = pe.value_load(flag[0:1, 0:1], min_val=0, max_val=1)
            with pe.If(ok == 0):
                with pe.Fori(0, slow_sweeps) as sweep:
                    pe.wait_ge(shs, sweep + 1)
                    transpose_h(1)
                    first = sweep * SEGL + STEPS
                    nth = sweep * (SEGL // 2) + STEPS // 2
                    inject(first, nth, 0)
                    with pe.Fori(0, SEGL // 2 - 1) as it:
                        pair(sweep * SEGL + it * 2 + STEPS, sweep * (SEGL // 2) + it + STEPS // 2, sweep + 1)
                    pair(sweep * SEGL + (STEPS + SEGL - 2), sweep * (SEGL // 2) + (STEPS // 2 + SEGL // 2 - 1),
                         sweep + 1, True)
                    shift_state()

            pe.wait_ge(segt, 1)
            mm(bank[6][0:SEGS, 0:D], before[0:SEGS, 0:SEGS], run, start=True, stop=True)
            mm(bank[6][0:SEGS, D:2 * D], ones[0:SEGS, 0:SEGS], run, start=True, stop=True).then_inc(segp, 1)



def kernel(**inputs):
    import numpy as np
    import concourse.bacc as bacc
    from concourse.bass_utils import run_bass_kernel_spmd as run

    def gates_first(a):
        return np.concatenate([a[2 * D:3 * D], a[0:D], a[D:2 * D], a[3 * D:4 * D]], axis=0)

    a = {k: np.asarray(val) for k, val in inputs.items()}
    consts = np.zeros((5, P, P), np.float32)
    consts[0] = np.eye(P)
    consts[1] = np.arange(P)[None, :]
    consts[2] = np.triu(np.ones((P, P)), 1)
    consts[3] = np.eye(P, k=1)
    consts[4] = 1.0
    arrays = {
        "x": a["x"], "src": a["src"], "dst": a["dst"], "edge_weight": a["edge_weight"],
        "w_gnn": a["L0_gnn_W_weight"].T, "b_gnn": a["L0_gnn_W_bias"],
        "w_ih": gates_first(a["L0_ffn_W_ih"]).T, "w_hh": gates_first(a["L0_ffn_W_hh"]).T,
        "b_ih": gates_first(a["L0_ffn_b_ih"]), "b_hh": gates_first(a["L0_ffn_b_hh"]),
        "w_lin": a["L0_ffn_W_lin"], "b_lin": a["L0_ffn_b_lin"],
        "fw": a["L0_ffn_fw_att"].reshape(D), "bw": a["L0_ffn_bw_att"].reshape(D),
        "consts": consts, "tile_iota": np.arange(TILES, dtype=np.float32),
    }
    arrays = {f"in_{k}": np.ascontiguousarray(val) for k, val in arrays.items()}
    nc = bacc.Bacc("TRN2", target_bir_lowering=False, num_devices=1)
    aps = {k[3:]: nc.dram_tensor(k, val.shape, mybir.dt.from_np(val.dtype), kind="ExternalInput").ap()
           for k, val in arrays.items()}
    out = nc.dram_tensor("out", (N, D), mybir.dt.float32, kind="ExternalOutput").ap()
    build(nc, aps, out)
    r = run(nc, [arrays], core_ids=[0])
    return r.results[0]["out"]
```

```python
from contextlib import ExitStack

import concourse.bass as bass
from concourse import mybir

N, D, E = 6250, 256, 100000
P = 128
G4 = 4 * D
EP, EC = 125, 800
NB = -(-N // P)
LASTB = N - (NB - 1) * P
TILES = (E + NB * (P - 1)) // P + 1
TU = 10
TILES = -(-TILES // TU) * TU
SEGS, SEGL = 125, 50
WARM = 74
SU = 16
BU = 7
CH = 160
NCH = EC // CH
XPR = WARM + N + WARM + SEGL
TOL = 2.0 ** -19
OU = 10
EPS = 1e-5
CLOSED = -1.0e4


def build(nc, A, out, slow_sweeps=SEGS - 1, tol=TOL):
    f32, i32, u8 = mybir.dt.float32, mybir.dt.int32, mybir.dt.uint8
    u32 = mybir.dt.uint32
    bf16 = mybir.dt.bfloat16
    ALU = mybir.AluOpType
    ACT = mybir.ActivationFunctionType
    AX = mybir.AxisListType
    ds = bass.ds
    RMAX = bass.bass_isa.ReduceOp.max

    sup_d = nc.dram_tensor("support_scratch", [NB * P, D], f32).ap()
    rec_d = nc.dram_tensor("record_scratch", [P * TILES, 3], f32).ap()
    xp_d = nc.dram_tensor("gate_input_scratch", [XPR, G4], f32).ap()
    x1_d = nc.dram_tensor("x1_scratch", [NB * P, D], f32).ap()

    with ExitStack() as ctx:
        def sb(name, shape, dt=f32):
            return ctx.enter_context(nc.sbuf_tensor(name, shape, dt))

        def pb(name, shape, dt=f32):
            return ctx.enter_context(nc.psum_tensor(name, shape, dt))

        def sem(name):
            return ctx.enter_context(nc.semaphore(name))

        big_a = sb("big_a", [P, NB + 1, D])
        big_b = sb("big_b", [P, NB + 1, D])
        big_c = sb("big_c", [P, NB + 1, D])
        consts = sb("consts_sb", [P, 5, P])
        ident, iota, before, shift, ones = (consts[:, i, :] for i in range(5))
        w_gnn = sb("w_gnn", [P, 2, D])
        b_gnn = sb("b_gnn", [P, D])
        w_ih = sb("w_ih", [P, 2, G4])
        b_ih = sb("b_ih_sb", [P, G4])
        w_lin = sb("w_lin", [P, 2, D])
        b_lin = sb("b_lin", [P, 2])
        fw = sb("fw", [P, D])
        bw = sb("bw", [P, D])
        records = sb("records", [P, TILES, 3])
        recs = records[:].rearrange("p t k -> p (t k)")[0:EP, 0:EC * 3].rearrange("p (c k) -> p c k", k=3)
        rec2 = records[:]
        posf = sb("posf", [EP, EC])
        num = sb("num", [EP, BU])
        cnt_g = sb("cnt_g", [EP, BU])
        cnt = sb("cnt", [EP, NB])
        pos0 = sb("pos0", [EP, NB])
        tot = sb("tot", [P, NB])
        tot_i = sb("tot_i", [P, NB], i32)
        tiles_f = sb("tiles_f", [P, NB])
        ends = sb("ends", [P, NB])
        ends_col = sb("ends_col", [NB, 1])
        table = sb("table", [1, TILES], i32)
        stg_i = sb("stg_i", [EP, 2, SU // 2], u32)
        stg_r = sb("stg_r", [EP, 2, SU // 2, 3])
        stg_g = sb("stg_g", [P, 2, TU // 2], u32)
        stg_w = sb("stg_w", [P, 2, TU // 2, 2])
        sums = sb("sums", [P, NB])
        var = sb("var", [P, NB])
        rstd = sb("rstd", [P, NB])
        tmp = sb("tmp", [P, NB])
        xn = sb("xn", [P, 2, D])
        xt = sb("xt", [P, 2, 2, P])
        pr = sb("pr", [P, 2, G4])
        gmax = sb("gmax", [P, 1])
        gall = sb("gall", [P, 1])
        flag = sb("flag", [1, 1], i32)

        spare = {"rank": big_b[:].rearrange("p b f -> p (b f)")}
        spare["later"] = big_c[:].rearrange("p b f -> p (b f)")
        taken = {"rank": 0, "later": 0}

        def part(stage, shape, dt=f32):
            size = 1
            for n in shape[1:]:
                size *= n
            at = taken[stage]
            taken[stage] += size
            view = spare[stage][0:shape[0], at:at + size]
            if dt != f32:
                view = view.bitcast(dt)
            if len(shape) == 3:
                view = view.rearrange("p (a b) -> p a b", a=shape[1])
            return view

        src_sb = part("rank", [EP, EC], i32)
        dst_sb = part("rank", [EP, EC], i32)
        bk_i = part("rank", [EP, EC], i32)
        pos_i = part("rank", [EP, EC], i32)
        w_sb = part("rank", [EP, EC])
        bk = part("rank", [EP, EC])
        mask = part("rank", [EP, BU * EC // 4]).bitcast(u8).rearrange("p (b c) -> p b c", b=BU)
        bk_c = part("rank", [EP, CH])
        pos_c = part("rank", [EP, CH])
        mask_c = part("rank", [EP, BU * CH // 4]).bitcast(u8).rearrange("p (b c) -> p b c", b=BU)
        cum = part("rank", [EP, BU, CH])
        pos_t = part("rank", [EP, CH], i32)
        row_t = part("rank", [EP, CH], i32)
        row_f = part("rank", [EP, CH])
        tile_iota = part("rank", [NB, TILES])
        tile_ge = part("rank", [NB, TILES])
        table_f = part("rank", [1, TILES])
        b_hh = part("later", [P, G4])
        rows = part("later", [P, TU, D])
        oneh = part("later", [P, TU, P])
        w_hh = part("later", [P, 2, G4])
        xp = part("later", [SEGS, 2, G4])
        h_s = part("later", [SEGS, 2, D])
        c_s = part("later", [SEGS, 2, D])
        start = part("later", [SEGS, 2, D])
        gap = part("later", [P, 2, D])
        h_t = part("later", [P, 2, SEGS])
        act_g, act_i, act_f, act_o, act_c = (part("later", [SEGS, D]) for _ in range(5))
        late = records[:].rearrange("p t k -> p (t k)")
        run, diff, base, ig, fc, t_h, t_w, t_s = (late[0:SEGS, i * D:(i + 1) * D] for i in range(8))
        dots = sb("dots", [SEGS, 2])
        dot0 = sb("dot0", [SEGS, 1])
        gate = sb("gate", [SEGS, 1])
        own = big_a[0:SEGS, 0:SEGL, :]
        x1s = big_b[0:SEGS, 0:SEGL, :]
        stats = sb("stats", [P, NB, 6])
        mean = sb("mean", [P, NB])

        bank = [pb(f"bank{i}", [P, 512]) for i in range(8)]

        load_w = sem("load_weights")
        load_c = sem("load_constants")
        load_e = sem("load_edges")
        load_x = sem("load_x")
        zeroed = sem("zeroed")
        rec_zero = sem("records_zeroed")
        v = sem("vector_chain")
        counted = sem("edges_counted")
        prefixed = sem("counts_prefixed")
        ends_r = sem("bucket_ends_ready")
        ends_t = sem("ends_transposed")
        ge_done = sem("tile_compare_done")
        table_s = sem("tile_blocks_summed")
        table_r = sem("tile_table_ready")
        placed = sem("edges_placed")
        staged = sem("scatter_staged")
        scat = [sem(f"scattered{i}") for i in range(2)]
        go = sem("gpsimd_may_issue")
        dgo = sem("vector_may_loop")
        ago = sem("scalar_may_loop")
        rec_l = sem("records_loaded")
        gst = sem("gather_staged")
        gat = [sem(f"gathered{i}") for i in range(TU)]
        oh_r = sem("onehot_ready")
        prod = sem("tile_product_done")
        added = sem("tile_added")
        var_r = sem("variance_ready")
        sq = sem("sqrt_done")
        cdone = sem("rows_centred")
        xn_r = sem("normalised_ready")
        xt_p = sem("transposed_in_psum")
        xt_r = sem("transposed_ready")
        pj = sem("projected")
        pr_r = sem("projection_copied")
        st0 = [sem(f"projection_stored{i}") for i in range(2)]
        xn_r2 = sem("normalised2_ready")
        xt_p2 = sem("transposed2_in_psum")
        xt_r2 = sem("transposed2_ready")
        pj2 = sem("projected2")
        pr_r2 = sem("projection2_copied")
        st2 = [sem(f"projection2_stored{i}") for i in range(2)]
        x1_r = sem("x1_ready")
        x1_st = sem("x1_stored")
        x1_ld = sem("x1_by_segment_loaded")
        pad_r = sem("pad_rows_ready")
        pad_s = sem("pad_rows_stored")
        xp_l = [sem(f"gate_input_loaded{i}") for i in range(2)]
        inj = sem("gate_input_in_psum")
        gi_r = sem("gates_gi_ready")
        f_r = sem("gate_f_ready")
        o_r = sem("gate_o_ready")
        a_gi = sem("act_gi_done")
        a_f = sem("act_f_done")
        a_o = sem("act_o_done")
        a_c = sem("tanh_c_done")
        s_m = sem("state_products_done")
        s_c = sem("c_ready")
        s_h = sem("h_ready")
        t_p = sem("h_transposed_in_psum")
        t_r = sem("h_transposed_ready")
        shf = sem("state_shifted")
        gapd = sem("gap_measured")
        gapa = sem("gap_over_all")
        flg = sem("flag_ready")
        shs = sem("shift_copied")
        o_v = sem("output_chain")
        segt = sem("segment_totals_ready")
        segp = sem("segment_prefix_done")
        res = sem("result_ready")
        out_s = sem("result_stored")

        block = ctx.enter_context(nc.Block())

        STEPS = WARM + SEGL
        TSLOW = STEPS + slow_sweeps * SEGL

        @block.sync
        def _(sp):
            sp.dma_start(src_sb, A["src"].rearrange("(p c) -> p c", p=EP)).then_inc(load_e, 16)
            sp.dma_start(dst_sb, A["dst"].rearrange("(p c) -> p c", p=EP)).then_inc(load_e, 16)
            sp.dma_start(w_sb, A["edge_weight"].rearrange("(p c) -> p c", p=EP)).then_inc(load_e, 16)
            sp.dma_start(consts[:], A["consts"].rearrange("k p f -> p k f")).then_inc(load_c, 16)
            sp.dma_start(tile_iota, A["tile_iota"].partition_broadcast(NB)).then_inc(load_c, 16)
            sp.wait_ge(zeroed, 1)
            sp.dma_start(big_a[:, 0:NB - 1, :], A["x"][0:(NB - 1) * P, :].rearrange("(b p) f -> p b f", p=P)
                         ).then_inc(load_x, 16)
            sp.dma_start(big_a[0:LASTB, NB - 1, :], A["x"][(NB - 1) * P:N, :]).then_inc(load_x, 16)
            sp.wait_ge(zeroed, 2)
            sp.dma_start(rec_d.rearrange("(p t) k -> p (t k)", p=P),
                         rec2.rearrange("p t k -> p (t k)")).then_inc(rec_zero, 16)
            for k, (name, tile) in enumerate([("w_gnn", w_gnn), ("w_ih", w_ih), ("w_hh", w_hh)]):
                sp.dma_start(tile[:, :, :], A[name].rearrange("(k p) f -> p k f", p=P)).then_inc(load_w, 16)
            sp.dma_start(b_gnn[:], A["b_gnn"].partition_broadcast(P)).then_inc(load_w, 16)
            sp.dma_start(b_ih[:], A["b_ih"].partition_broadcast(P)).then_inc(load_w, 16)
            sp.dma_start(b_hh, A["b_hh"].partition_broadcast(P)).then_inc(load_w, 16)
            for l in range(2):
                sp.dma_start(w_lin[:, l, :], A["w_lin"][l, :].partition_broadcast(P)).then_inc(load_w, 16)
            sp.dma_start(b_lin[:], A["b_lin"].partition_broadcast(P)).then_inc(load_w, 16)
            sp.dma_start(fw[:], A["fw"].partition_broadcast(P)).then_inc(load_w, 16)
            sp.dma_start(bw[:], A["bw"].partition_broadcast(P)).then_inc(load_w, 16)

            def store_support(t, q, nth):
                first = sp.snap(t * P) if not isinstance(t, int) else t * P
                sp.wait_ge(pr_r, t + 1)
                sp.dma_start(sup_d[ds(first, P), :], pr[:, q, 0:D]).then_inc(st0[q], 16)

            with sp.Fori(0, NB // 2) as it:
                store_support(it * 2, 0, it)
                store_support(it * 2 + 1, 1, it)
            store_support(NB - 1, 0, NB // 2)

            for q in range(2):
                sp.wait_ge(scat[q], 16 * EC // 2)
            sp.dma_start(rec2.rearrange("p t k -> p (t k)"),
                         rec_d.rearrange("(p t) k -> p (t k)", p=P)).then_inc(rec_l, 16)

            sp.wait_ge(pad_r, 1)
            sp.dma_start(xp_d[0:WARM, :], pr[0:WARM, 0, :]).then_inc(pad_s, 16)
            sp.wait_ge(x1_r, 1)
            sp.dma_start(x1_d.rearrange("(b p) f -> p b f", p=P), big_b[:, 0:NB, :]).then_inc(x1_st, 16)

            def store_gate_input(t, q):
                first = sp.snap(t * P + WARM) if not isinstance(t, int) else t * P + WARM
                sp.wait_ge(pr_r2, t + 1)
                sp.dma_start(xp_d[ds(first, P), :], pr[:, q, :]).then_inc(st2[q], 16)

            sp.wait_ge(pad_s, 16)
            with sp.Fori(0, NB // 2) as it:
                store_gate_input(it * 2, 0)
                store_gate_input(it * 2 + 1, 1)
            store_gate_input(NB - 1, 0)
            sp.wait_ge(st2[0], 16 * (NB // 2 + 1))
            sp.wait_ge(st2[1], 16 * (NB // 2))
            sp.wait_ge(x1_st, 16)
            sp.dma_start(x1s, x1_d[0:N, :].rearrange("(k l) f -> k l f", l=SEGL)).then_inc(x1_ld, 16)

            def load_gate_input(u, t, q, first=False):
                row = t if isinstance(t, int) else sp.snap(t)
                if not first:
                    sp.wait_ge(inj, u - 1)
                sp.dma_start(xp[:, q, :], xp_d[ds(row, SEGS, step=SEGL), :]).then_inc(xp_l[q], 16)

            load_gate_input(0, 0, 0, True)
            load_gate_input(1, 1, 1, True)
            with sp.Fori(1, STEPS // 2) as it:
                load_gate_input(it * 2, it * 2, 0)
                load_gate_input(it * 2 + 1, it * 2 + 1, 1)
            sp.wait_ge(flg, 1)
            ok = sp.value_load(flag[0:1, 0:1], min_val=0, max_val=1)
            with sp.If(ok == 0):
                with sp.Fori(0, slow_sweeps) as sweep:
                    with sp.Fori(0, SEGL // 2) as it:
                        for q in range(2):
                            load_gate_input(sweep * SEGL + it * 2 + (STEPS + q), it * 2 + (WARM + q), q)

            for i in range(SEGL // OU):
                sp.wait_ge(res, i + 1)
                sp.dma_start(out.rearrange("(k l) f -> k l f", l=SEGL)[:, i * OU:(i + 1) * OU, :],
                             own[:, i * OU:(i + 1) * OU, :]).then_inc(out_s, 16)
            sp.wait_ge(out_s, 16 * (SEGL // OU))

        @block.gpsimd
        def _(pool):
            nc.gpsimd.memset(big_a[:, NB - 1, :], 0.0).then_inc(zeroed, 1)
            nc.gpsimd.memset(rec2, 0.0).then_inc(zeroed, 1)
            pool.wait_ge(rec_zero, 16)
            HU = SU // 2

            with pool.Fori(0, EC // SU) as it:
                for q in range(2):
                    pool.wait_ge(staged, it * 2 + (q + 1))
                    pool.sem_inc(go, 1)
                    for j in range(HU):
                        pool.indirect_dma_start(
                            out=rec_d, out_offset=bass.IndirectOffsetOnAxis(ap=stg_i[:, q, j:j + 1], axis=0),
                            in_=stg_r[:, q, j, :], in_offset=None).then_inc(scat[q], 16)

            GU = TU // 2
            for q in range(2):
                pool.wait_ge(st0[q], 16 * (NB // 2 + 1 - q))

            def gather(it):
                for q in range(2):
                    pool.wait_ge(gst, it * 2 + (q + 1))
                    pool.sem_inc(go, 1)
                    for j in range(GU):
                        s = q * GU + j
                        pool.indirect_dma_start(
                            out=rows[:, s, :], out_offset=None, in_=sup_d,
                            in_offset=bass.IndirectOffsetOnAxis(ap=stg_g[:, q, j:j + 1], axis=0)
                        ).then_inc(gat[s], 16)

            with pool.Fori(0, TILES // TU) as it:
                gather(it)

            pool.wait_ge(gapd, 1)
            nc.gpsimd.partition_all_reduce(gall[:], gmax[:], P, RMAX).then_inc(gapa, 1)

        @block.scalar
        def _(act):
            HU = SU // 2
            GU = TU // 2

            def stage_scatter(it, q, first=False):
                if not first:
                    act.wait_ge(scat[q], it * (16 * HU))
                nc.scalar.copy(stg_i[:, q, :], posf[:, ds(it * SU + q * HU, HU)])
                nc.scalar.copy(stg_r[:, q, :, :], recs[:, ds(it * SU + q * HU, HU), :]).then_inc(staged, 1)

            def sqrt_var(nth):
                act.wait_ge(var_r, nth)
                nc.scalar.activation(tmp[:], var[:], ACT.Sqrt).then_inc(sq, 1)

            def copy_transposed(t, q, ready, used, out_ready, first=False):
                act.wait_ge(ready, t + 1)
                if not first:
                    act.wait_ge(used, t - 1)
                nc.scalar.copy(xt[:, q, :, :], bank[q][:, 0:2 * P].rearrange("p (k n) -> p k n", k=2)
                               ).then_inc(out_ready, 1)

            PER = CH // SU
            act.wait_ge(placed, 1)
            stage_scatter(0, 0, True)
            stage_scatter(0, 1, True)
            with act.Fori(1, PER) as it:
                stage_scatter(it, 0)
                stage_scatter(it, 1)
            act.wait_ge(placed, 2)
            with act.Fori(PER, 2 * PER) as it:
                stage_scatter(it, 0)
                stage_scatter(it, 1)
            sqrt_var(1)
            with act.Fori(2, NCH) as c:
                act.wait_ge(placed, c + 1)
                act.sem_inc(ago, 1)
                with act.Fori(0, PER) as i:
                    stage_scatter(c * PER + i, 0)
                    stage_scatter(c * PER + i, 1)

            def stage_gather(it, q, first=False):
                if not first:
                    act.wait_ge(prod, it * TU + (q * GU + GU - TU))
                src = rec2[:, ds(it * TU + q * GU, GU), :]
                nc.scalar.copy(stg_g[:, q, :], src[:, :, 0])
                nc.scalar.copy(stg_w[:, q, :, :], src[:, :, 1:3]).then_inc(gst, 1)

            act.wait_ge(rec_l, 16)
            stage_gather(0, 0, True)
            stage_gather(0, 1, True)
            with act.Fori(1, TILES // TU) as it:
                stage_gather(it, 0)
                stage_gather(it, 1)

            sqrt_var(2)
            copy_transposed(0, 0, xt_p2, pj2, xt_r2, True)
            copy_transposed(1, 1, xt_p2, pj2, xt_r2, True)
            with act.Fori(1, NB // 2) as it:
                copy_transposed(it * 2, 0, xt_p2, pj2, xt_r2)
                copy_transposed(it * 2 + 1, 1, xt_p2, pj2, xt_r2)
            copy_transposed(NB - 1, 0, xt_p2, pj2, xt_r2)

            def step(u, q):
                act.wait_ge(gi_r, u + 1)
                nc.scalar.activation(act_g, bank[3 * q][0:SEGS, 0:D], ACT.Tanh)
                nc.scalar.activation(act_i, bank[3 * q][0:SEGS, D:2 * D], ACT.Sigmoid).then_inc(a_gi, 1)
                act.wait_ge(f_r, u + 1)
                nc.scalar.activation(act_f, bank[3 * q + 1][0:SEGS, 0:D], ACT.Sigmoid).then_inc(a_f, 1)
                act.wait_ge(o_r, u + 1)
                nc.scalar.activation(act_o, bank[3 * q + 2][0:SEGS, 0:D], ACT.Sigmoid).then_inc(a_o, 1)
                act.wait_ge(s_c, u + 1)
                nc.scalar.activation(act_c, c_s[:, q, :], ACT.Tanh).then_inc(a_c, 1)

            with act.Fori(0, STEPS // 2) as it:
                step(it * 2, 0)
                step(it * 2 + 1, 1)
            act.wait_ge(flg, 1)
            ok = act.value_load(flag[0:1, 0:1], min_val=0, max_val=1)
            with act.If(ok == 0):
                with act.Fori(0, slow_sweeps) as sweep:
                    with act.Fori(0, SEGL // 2) as it:
                        for q in range(2):
                            step(sweep * SEGL + it * 2 + (STEPS + q), q)

        @block.vector
        def _(dve):
            count = [0]

            def link(ins):
                count[0] += 1
                ins.then_inc(v, 1)
                dve.wait_ge(v, count[0])

            V = nc.vector
            dve.wait_ge(load_e, 48)
            V.tensor_scalar(bk_i, src_sb, 7, None, ALU.arith_shift_right)
            link(V.tensor_scalar(pos_i, src_sb, P - 1, None, ALU.bitwise_and))
            dve.wait_ge(rec_zero, 16)
            V.tensor_copy(recs[:, :, 2], pos_i)
            V.tensor_copy(recs[:, :, 1], w_sb)
            V.tensor_copy(recs[:, :, 0], dst_sb)
            link(V.tensor_copy(bk, bk_i))
            dve.wait_ge(load_c, 32)
            with dve.Fori(0, NB // BU) as g:
                n = g * 3 + count[0]
                V.tensor_scalar(num[:], iota[0:EP, ds(g * BU, BU)], 0.0, None, ALU.add).then_inc(v, 1)
                dve.wait_ge(v, n + 1)
                for b in range(BU):
                    ins = V.tensor_scalar(mask[:, b, :], bk, num[:, b:b + 1], 0.0, ALU.is_equal, ALU.add,
                                          accum_out=cnt_g[:, b:b + 1])
                ins.then_inc(v, 1)
                dve.wait_ge(v, n + 2)
                V.tensor_scalar(cnt[:, ds(g * BU, BU)], cnt_g[:], 0.0, None, ALU.add).then_inc(v, 1)
                dve.wait_ge(v, n + 3)
            count[0] += 3 * (NB // BU)
            V.memset(pos_c, 0.0).then_inc(counted, 1)
            dve.wait_ge(prefixed, 1)
            link(V.tensor_copy(tot[:], bank[0][:, 0:NB]))
            link(V.tensor_scalar(tot_i[:], tot[:], float(P - 1), None, ALU.add))
            link(V.tensor_scalar(tot_i[:], tot_i[:], 7, None, ALU.arith_shift_right))
            link(V.tensor_copy(tiles_f[:], tot_i[:]))
            link(V.tensor_tensor_scan(ends[:], tiles_f[:], tiles_f[:], 0.0, ALU.add, ALU.bypass))
            link(V.tensor_tensor(tmp[:], ends[:], tiles_f[:], ALU.subtract))
            link(V.tensor_scalar(tmp[:], tmp[:], float(P), -1.0, ALU.mult, ALU.add))
            V.tensor_tensor(pos0[:], tmp[0:EP, :], bank[1][0:EP, 0:NB], ALU.add).then_inc(ends_r, 1)
            dve.wait_ge(ends_r, 1)

            def wide(a):
                return a.rearrange("p (o c) -> p o c", o=1).broadcast_to([EP, BU, CH])

            def deep(a):
                return a.rearrange("p (b o) -> p b o", o=1).broadcast_to([EP, BU, CH])

            def rank(first, last):
                per_g = 3 + BU
                each = (NB // BU) * per_g + 6
                with dve.Fori(first, last) as c:
                    m = (c - first) * each + count[0]
                    V.tensor_scalar(bk_c, bk[:, ds(c * CH, CH)], 0.0, None, ALU.add).then_inc(v, 1)
                    dve.wait_ge(v, m + 1)
                    dve.sem_inc(dgo, 1)
                    with dve.Fori(0, NB // BU) as g:
                        n = (c - first) * each + g * per_g + (count[0] + 1)
                        V.tensor_tensor(mask_c, wide(bk_c), deep(iota[0:EP, ds(g * BU, BU)]), ALU.is_equal
                                        ).then_inc(v, 1)
                        dve.wait_ge(v, n + 1)
                        for b in range(BU):
                            ins = V.tensor_tensor_scan(cum[:, b, :], mask_c[:, b, :], mask_c[:, b, :],
                                                       pos0[:, ds(g * BU + b, 1)], ALU.add, ALU.bypass)
                        ins.then_inc(v, 1)
                        dve.wait_ge(v, n + 2)
                        V.tensor_scalar(pos0[:, ds(g * BU, BU)], cum[:, :, CH - 1], 0.0, None, ALU.add).then_inc(v, 1)
                        for b in range(BU):
                            V.copy_predicated(pos_c, mask_c[:, b, :], cum[:, b, :]).then_inc(v, 1)
                            dve.wait_ge(v, n + (b + 4))
                            dve.sem_inc(dgo, 1)
                    n = (c - first) * each + (count[0] + each - 5)
                    V.tensor_copy(pos_t, pos_c).then_inc(v, 1)
                    dve.wait_ge(v, n + 1)
                    V.tensor_scalar(row_t, pos_t, 7, None, ALU.arith_shift_right).then_inc(v, 1)
                    dve.wait_ge(v, n + 2)
                    V.tensor_copy(row_f, row_t).then_inc(v, 1)
                    V.tensor_scalar(pos_t, pos_t, P - 1, None, ALU.bitwise_and).then_inc(v, 1)
                    dve.wait_ge(v, n + 4)
                    V.scalar_tensor_tensor(posf[:, ds(c * CH, CH)], pos_t, float(TILES), row_f, ALU.mult, ALU.add
                                           ).then_inc(placed, 1)
                    dve.wait_ge(placed, c + 1)
                    dve.sem_inc(v, 1)
                count[0] += each * (last - first)

            rank(0, 2)

            dve.wait_ge(ends_t, 1)
            link(V.tensor_copy(ends_col[:], bank[2][0:NB, 0:1]))
            V.tensor_scalar(tile_ge, tile_iota, ends_col[:, 0:1], None, ALU.is_ge).then_inc(ge_done, 1)
            dve.wait_ge(table_s, 1)
            V.tensor_scalar(table_f[0:1, 0:512], bank[3][0:1, 0:512], float(NB - 1), float(D), ALU.min, ALU.mult)
            link(V.tensor_scalar(table_f[0:1, 512:TILES], bank[4][0:1, 0:TILES - 512], float(NB - 1), float(D),
                                 ALU.min, ALU.mult))
            link(V.tensor_copy(table[:], table_f))

            def norm(rowsin, nth):
                with dve.Fori(0, NB) as b:
                    V.bn_stats(stats[:, ds(b, 1), :].rearrange("p o k -> p (o k)"),
                               rowsin[:, ds(b, 1), :].rearrange("p o f -> p (o f)"))
                link(V.memset(ends_col[:], 0.0))
                even, odd = stats[:, :, 1], stats[:, :, 4]
                V.tensor_tensor(mean[:], even, odd, ALU.add)
                V.tensor_tensor(var[:], stats[:, :, 2], stats[:, :, 5], ALU.add)
                link(V.tensor_tensor(sums[:], even, odd, ALU.subtract))
                V.tensor_scalar(mean[:], mean[:], 0.5, None, ALU.mult)
                link(V.tensor_tensor(sums[:], sums[:], sums[:], ALU.mult))
                link(V.scalar_tensor_tensor(var[:], sums[:], D / 4.0, var[:], ALU.mult, ALU.add))
                V.tensor_scalar(var[:], var[:], 1.0 / D, EPS, ALU.mult, ALU.add).then_inc(var_r, 1)
                dve.wait_ge(sq, nth)
                link(V.reciprocal(rstd[:], tmp[:]))
                link(V.tensor_tensor(tmp[:], rstd[:], rstd[:], ALU.mult))
                link(V.tensor_tensor(tmp[:], tmp[:], var[:], ALU.mult))
                link(V.tensor_scalar(tmp[:], tmp[:], -0.5, 1.5, ALU.mult, ALU.add))
                link(V.tensor_tensor(rstd[:], rstd[:], tmp[:], ALU.mult))

            def normalise(rowsin, t, q, ready, free, first=False):
                if not first:
                    dve.wait_ge(free, t - 1)
                V.tensor_scalar(xn[:, q:q + 1, :], rowsin[:, ds(t, 1), :], mean[:, ds(t, 1)], rstd[:, ds(t, 1)],
                                ALU.subtract, ALU.mult).then_inc(ready, 1)

            def copy_transposed(t, q):
                dve.wait_ge(xt_p, t + 1)
                V.tensor_copy(xt[:, q, :, :], bank[q][:, 0:2 * P].rearrange("p (k n) -> p k n", k=2)
                              ).then_inc(xt_r, 1)

            def evacuate_support(t, q, first=False):
                dve.wait_ge(pj, t + 1)
                if not first:
                    dve.wait_ge(st0[q], t * 8 - q * 8)
                V.tensor_tensor(pr[:, q, 0:D], bank[2 + q][:, 0:D], b_gnn[:], ALU.add).then_inc(pr_r, 1)

            dve.wait_ge(load_x, 32)
            dve.wait_ge(zeroed, 1)
            norm(big_a[:, 0:NB, :], 1)
            rank(2, NCH)
            link(V.memset(big_b[:], 0.0))
            dve.wait_ge(load_w, 16 * 11)
            V.tensor_tensor(b_ih[:], b_ih[:], b_hh, ALU.add)
            normalise(big_a, 0, 0, xn_r, xt_p, True)
            normalise(big_a, 1, 1, xn_r, xt_p, True)
            copy_transposed(0, 0)
            copy_transposed(1, 1)
            normalise(big_a, 2, 0, xn_r, xt_p)
            evacuate_support(0, 0, True)
            copy_transposed(2, 0)
            normalise(big_a, 3, 1, xn_r, xt_p)
            evacuate_support(1, 1, True)
            copy_transposed(3, 1)

            def support_pair(t):
                for q in range(2):
                    normalise(big_a, t + (q + 2), q, xn_r, xt_p)
                    evacuate_support(t + q, q)
                    copy_transposed(t + (q + 2), q)

            with dve.Fori(1, NB // 2 - 1) as it:
                support_pair(it * 2)
            normalise(big_a, NB - 1, 0, xn_r, xt_p)
            evacuate_support(NB - 3, 0)
            copy_transposed(NB - 1, 0)
            evacuate_support(NB - 2, 1)
            evacuate_support(NB - 1, 0)
            dve.wait_ge(st0[0], 16 * (NB // 2 + 1))
            dve.wait_ge(st0[1], 16 * (NB // 2))
            link(V.memset(pr[:], 0.0))
            V.memset(pr[0:WARM, 0, D:2 * D], CLOSED)
            V.memset(pr[0:WARM, 0, 3 * D:4 * D], CLOSED).then_inc(pad_r, 1)

            GU = TU // 2
            regs = [dve.alloc_register(f"tile_block{s}") for s in range(TU)]
            acc = big_b[:].rearrange("p b f -> p (b f)")

            def onehots(it, q):
                dve.wait_ge(gst, it * 2 + q + 1)
                for j in range(GU):
                    s = q * GU + j
                    V.tensor_scalar(oneh[:, s, :], iota[:], stg_w[:, q, j, 1:2], stg_w[:, q, j, 0:1],
                                    ALU.is_equal, ALU.mult).then_inc(oh_r, 1)

            def add_tiles(it, q, vals):
                for j in range(GU):
                    s = q * GU + j
                    dve.wait_ge(prod, it * TU + (s + 1))
                    at = acc[:, ds(vals[s], D)]
                    V.tensor_tensor(at, at, bank[s % 2][:, 0:D], ALU.add).then_inc(added, 1)
                    dve.wait_ge(added, it * TU + (s + 1))

            onehots(0, 0)
            def blocks(it):
                dve.reg_load(regs, table[0:1, ds(it * TU, TU)])
                return [dve.snap(r, min_val=0, max_val=(NB - 1) * D) for r in regs]
            with dve.Fori(0, TILES // TU - 1) as it:
                vals = blocks(it)
                onehots(it, 1)
                add_tiles(it, 0, vals)
                onehots(it + 1, 0)
                add_tiles(it, 1, vals)
            last = TILES // TU - 1
            vals = blocks(last)
            onehots(last, 1)
            add_tiles(last, 0, vals)
            add_tiles(last, 1, vals)

            dve.wait_ge(pad_s, 16)
            V.tensor_tensor(big_b[:, 0:NB, :], big_b[:, 0:NB, :], big_a[:, 0:NB, :], ALU.add).then_inc(x1_r, 1)
            dve.wait_ge(x1_r, 1)
            norm(big_b[:, 0:NB, :], 2)

            def evacuate_gates(t, q, first=False):
                dve.wait_ge(pj2, t + 1)
                if not first:
                    dve.wait_ge(st2[q], t * 8 - q * 8)
                for c in range(2):
                    last = V.tensor_tensor(pr[:, q, c * 512:c * 512 + 512], bank[2 + 2 * q + c][:],
                                           b_ih[:, c * 512:c * 512 + 512], ALU.add)
                last.then_inc(pr_r2, 1)

            dve.wait_ge(pad_s, 16)
            normalise(big_b, 0, 0, xn_r2, xt_p2, True)
            normalise(big_b, 1, 1, xn_r2, xt_p2, True)
            normalise(big_b, 2, 0, xn_r2, xt_p2)
            evacuate_gates(0, 0, True)
            normalise(big_b, 3, 1, xn_r2, xt_p2)
            evacuate_gates(1, 1, True)
            with dve.Fori(1, NB // 2 - 1) as it:
                for q in range(2):
                    normalise(big_b, it * 2 + (q + 2), q, xn_r2, xt_p2)
                    evacuate_gates(it * 2 + q, q)
            normalise(big_b, NB - 1, 0, xn_r2, xt_p2)
            evacuate_gates(NB - 3, 0)
            evacuate_gates(NB - 2, 1)
            evacuate_gates(NB - 1, 0)
            V.tensor_tensor(diff, fw[0:SEGS, :], bw[0:SEGS, :], ALU.subtract)

            V.memset(gap, 0.0)
            V.memset(c_s, 0.0).then_inc(s_m, 1)
            V.memset(h_t, 0.0).then_inc(t_r, 1)
            dve.wait_ge(s_m, 1)

            def step(u, q, extra, j=None, done=None):
                dve.wait_ge(a_gi, u + 1)
                V.tensor_tensor(ig, act_g, act_i, ALU.mult).then_inc(s_m, 1)
                dve.wait_ge(a_f, u + 1)
                V.tensor_tensor(fc, act_f, c_s[:, 1 - q, :], ALU.mult).then_inc(s_m, 1)
                dve.wait_ge(s_m, u * 2 + 3)
                V.tensor_tensor(c_s[:, q, :], ig, fc, ALU.add).then_inc(s_c, 1)
                dve.wait_ge(a_c, u + 1)
                V.tensor_tensor(h_s[:, q, :], act_o, act_c, ALU.mult).then_inc(s_h, 1)
                copy_h(u + extra)
                if j is not None:
                    outputs(j, q, done)

            def copy_h(n):
                dve.wait_ge(t_p, n + 1)
                V.tensor_copy(h_t, bank[6][:, 0:2 * P].rearrange("p (k n) -> p k n", k=2)[:, :, 0:SEGS]
                              ).then_inc(t_r, 1)

            OPS = 8

            def outputs(j, q, done):
                n = done * OPS
                h = h_s[:, q, :]
                at = own[:, ds(j, 1), :].rearrange("k l f -> k (l f)")
                for l in range(2):
                    ins = V.tensor_tensor_reduce(out=t_w if l else t_s, in0=h, in1=w_lin[0:SEGS, l, :], scale=1.0,
                                                 scalar=0.0, op0=ALU.mult, op1=ALU.add, accum_out=dots[:, l:l + 1])
                ins.then_inc(o_v, 1)
                V.scalar_tensor_tensor(t_h, h, 2.0, x1s[:, ds(j, 1), :].rearrange("k l f -> k (l f)"),
                                       ALU.mult, ALU.add).then_inc(o_v, 1)
                dve.wait_ge(o_v, n + 1)
                V.tensor_tensor(dot0[:], dots[:, 0:1], b_lin[0:SEGS, 0:1], ALU.add).then_inc(o_v, 1)
                dve.wait_ge(o_v, n + 3)
                V.scalar_tensor_tensor(gate[:], dots[:, 1:2], b_lin[0:SEGS, 1:2], dot0[:], ALU.add, ALU.is_gt
                                       ).then_inc(o_v, 1)
                dve.wait_ge(o_v, n + 4)
                V.scalar_tensor_tensor(run, h, gate[:, 0:1], run, ALU.mult, ALU.add).then_inc(o_v, 1)
                V.scalar_tensor_tensor(t_w, h, gate[:, 0:1], fw[0:SEGS, :], ALU.mult, ALU.mult).then_inc(o_v, 1)
                dve.wait_ge(o_v, n + 6)
                V.tensor_tensor(t_s, run, diff, ALU.mult)
                V.tensor_tensor(t_h, t_h, t_w, ALU.subtract).then_inc(o_v, 1)
                dve.wait_ge(o_v, n + 7)
                V.tensor_tensor(at, t_h, t_s, ALU.add).then_inc(o_v, 1)

            with dve.Fori(0, WARM // 2) as it:
                step(it * 2, 0, 0)
                step(it * 2 + 1, 1, 0)
            V.tensor_copy(start[:, 0, :], h_s[:, 1, :])
            V.tensor_copy(start[:, 1, :], c_s[:, 1, :])
            link(V.memset(run, 0.0))
            dve.wait_ge(x1_ld, 16)
            with dve.Fori(0, SEGL // 2) as it:
                for q in range(2):
                    step(it * 2 + (WARM + q), q, 0, it * 2 + q, it * 2 + q)

            dve.wait_ge(shf, 1)
            for k in range(2):
                ins = V.tensor_tensor(gap[0:SEGS, k, :], bank[7][0:SEGS, k * D:(k + 1) * D], start[:, k, :],
                                      ALU.subtract)
            link(ins)
            V.tensor_reduce(gmax[:], gap, AX.XY, ALU.max, apply_absolute_value=True).then_inc(gapd, 1)
            dve.wait_ge(gapa, 1)
            V.tensor_scalar(flag[:], gall[0:1, :], tol, None, ALU.is_le).then_inc(flg, 1)
            dve.wait_ge(flg, 1)
            ok = dve.value_load(flag[0:1, 0:1], min_val=0, max_val=1)
            with dve.If(ok == 0):
                with dve.Fori(0, slow_sweeps) as sweep:
                    dve.wait_ge(shf, sweep + 1)
                    dve.wait_ge(o_v, sweep * (SEGL * OPS) + SEGL * OPS)
                    V.memset(run, 0.0)
                    V.tensor_copy(h_s[:, 1, :], bank[7][0:SEGS, 0:D])
                    V.tensor_copy(c_s[:, 1, :], bank[7][0:SEGS, D:2 * D]).then_inc(shs, 1)
                    dve.wait_ge(shs, sweep + 1)
                    copy_h(sweep * (SEGL + 1) + STEPS)
                    dve.sem_inc(dgo, 1)
                    with dve.Fori(0, SEGL // 2) as it:
                        for q in range(2):
                            step(sweep * SEGL + it * 2 + (STEPS + q), q, sweep + 1,
                                 it * 2 + q, sweep * SEGL + it * 2 + (SEGL + q))

                dve.wait_ge(shf, slow_sweeps + 1)
                dve.wait_ge(t_r, STEPS + slow_sweeps * (SEGL + 1) + 1)
                dve.wait_ge(o_v, SEGL * OPS * (slow_sweeps + 1))
                dve.sem_inc(dgo, 1)

            dve.wait_ge(o_v, SEGL * OPS)
            V.memset(dot0[:], 0.0).then_inc(segt, 1)
            dve.wait_ge(segp, 1)
            V.tensor_tensor(base, bank[6][0:SEGS, D:2 * D], bw[0:SEGS, :], ALU.mult)
            link(V.tensor_tensor(t_s, bank[6][0:SEGS, 0:D], diff, ALU.mult))
            link(V.tensor_tensor(base, base, t_s, ALU.add))
            for i in range(SEGL // OU):
                part_o = own[:, i * OU:(i + 1) * OU, :]
                V.tensor_tensor(part_o, part_o, base.rearrange("k (o f) -> k o f", o=1).broadcast_to([SEGS, OU, D]),
                                ALU.add).then_inc(res, 1)

        @block.tensor
        def _(pe):
            mm = nc.tensor.matmul
            pe.wait_ge(load_c, 32)
            pe.wait_ge(counted, 1)
            mm(bank[1][0:EP, 0:NB], before[0:EP, 0:EP], cnt[:], start=True, stop=True)
            mm(bank[0][:, 0:NB], ones[0:EP, :], cnt[:], start=True, stop=True).then_inc(prefixed, 1)
            pe.wait_ge(ends_r, 1)
            mm(bank[2][0:NB, 0:1], ends[0:1, :], ones[0:1, 0:1], start=True, stop=True).then_inc(ends_t, 1)
            pe.wait_ge(ge_done, 1)
            mm(bank[3][0:1, 0:512], ones[0:NB, 0:1], tile_ge[:, 0:512], start=True, stop=True)
            mm(bank[4][0:1, 0:TILES - 512], ones[0:NB, 0:1], tile_ge[:, 512:TILES], start=True, stop=True
               ).then_inc(table_s, 1)

            def transpose_rows(t, q, ready, copied, done, first=False):
                pe.wait_ge(ready, t + 1)
                if not first:
                    pe.wait_ge(copied, t - 1)
                for k in range(2):
                    ins = nc.tensor.transpose(bank[q][:, k * P:(k + 1) * P], xn[:, q, k * P:(k + 1) * P], ident[:])
                ins.then_inc(done, 1)

            def project_support(t, q, first=False):
                pe.wait_ge(xt_r, t + 1)
                if not first:
                    pe.wait_ge(pr_r, t - 1)
                for k in range(2):
                    ins = mm(bank[2 + q][:, 0:D], xt[:, q, k, :], w_gnn[:, k, :], start=k == 0, stop=k == 1)
                ins.then_inc(pj, 1)

            def project_gates(t, q, first=False):
                pe.wait_ge(xt_r2, t + 1)
                if not first:
                    pe.wait_ge(pr_r2, t - 1)
                for c in range(2):
                    for k in range(2):
                        ins = mm(bank[2 + 2 * q + c][:], xt[:, q, k, :], w_ih[:, k, c * 512:(c + 1) * 512],
                                 start=k == 0, stop=k == 1)
                ins.then_inc(pj2, 1)

            def all_blocks(project, ready, copied, done):
                transpose_rows(0, 0, ready, copied, done, True)
                transpose_rows(1, 1, ready, copied, done, True)
                project(0, 0, True)
                transpose_rows(2, 0, ready, copied, done)
                project(1, 1, True)
                transpose_rows(3, 1, ready, copied, done)
                with pe.Fori(1, NB // 2 - 1) as it:
                    project(it * 2, 0)
                    transpose_rows(it * 2 + 2, 0, ready, copied, done)
                    project(it * 2 + 1, 1)
                    transpose_rows(it * 2 + 3, 1, ready, copied, done)
                project(NB - 3, 0)
                transpose_rows(NB - 1, 0, ready, copied, done)
                project(NB - 2, 1)
                project(NB - 1, 0)

            pe.wait_ge(load_w, 16 * 11)
            all_blocks(project_support, xn_r, xt_r, xt_p)

            def tile_products(it, first=False):
                for s in range(TU):
                    pe.wait_ge(oh_r, it * TU + (s + 1))
                    pe.wait_ge(gat[s], it * 16 + 16)
                    if not (first and s < 2):
                        pe.wait_ge(added, it * TU + (s - 1))
                    mm(bank[s % 2][:, 0:D], oneh[:, s, :], rows[:, s, :], start=True, stop=True).then_inc(prod, 1)

            tile_products(0, True)
            with pe.Fori(1, TILES // TU) as it:
                tile_products(it)

            all_blocks(project_gates, xn_r2, xt_r2, xt_p2)

            PARTS = ((0, 0, 2 * D, gi_r), (1, 2 * D, D, f_r), (2, 3 * D, D, o_r))

            def inject(u, nth, q, first=False):
                pe.wait_ge(xp_l[q], nth * 16 + 16)
                if not first:
                    pe.wait_ge(a_o, u - 1)
                for c, at, width, _ in PARTS:
                    ins = mm(bank[3 * q + c][0:SEGS, 0:width], ident[0:SEGS, 0:SEGS], xp[:, q, at:at + width],
                             start=True, stop=False)
                ins.then_inc(inj, 1)

            def recur(u, q, extra):
                pe.wait_ge(t_r, u + extra + 1)
                for c, at, width, ready in PARTS:
                    for k in range(2):
                        ins = mm(bank[3 * q + c][0:SEGS, 0:width], h_t[:, k, :], w_hh[:, k, at:at + width],
                                 start=False, stop=k == 1)
                    ins.then_inc(ready, 1)

            def transpose_h(q):
                for k in range(2):
                    ins = nc.tensor.transpose(bank[6][:, k * P:k * P + SEGS], h_s[:, q, k * P:(k + 1) * P],
                                              ident[0:SEGS, 0:SEGS])
                ins.then_inc(t_p, 1)

            def shift_state():
                for k, state in enumerate((h_s, c_s)):
                    ins = mm(bank[7][0:SEGS, k * D:(k + 1) * D], shift[0:SEGS, 0:SEGS], state[:, 1, :],
                             start=True, stop=True)
                ins.then_inc(shf, 1)

            def pair(u, nth, extra, last=False):
                for q in range(2):
                    recur(u + q, q, extra)
                    if not (last and q):
                        inject(u + (q + 1), nth + q, 1 - q)
                    pe.wait_ge(s_h, u + (q + 1))
                    transpose_h(q)

            pe.wait_ge(pr_r2, NB)
            inject(0, 0, 0, True)
            recur(0, 0, 0)
            inject(1, 0, 1, True)
            pe.wait_ge(s_h, 1)
            transpose_h(0)
            recur(1, 1, 0)
            inject(2, 1, 0)
            pe.wait_ge(s_h, 2)
            transpose_h(1)
            with pe.Fori(1, STEPS // 2 - 1) as it:
                pair(it * 2, it, 0)
            pair(STEPS - 2, STEPS // 2 - 1, 0, True)
            shift_state()
            pe.wait_ge(flg, 1)
            ok = pe.value_load(flag[0:1, 0:1], min_val=0, max_val=1)
            with pe.If(ok == 0):
                with pe.Fori(0, slow_sweeps) as sweep:
                    pe.wait_ge(shs, sweep + 1)
                    transpose_h(1)
                    first = sweep * SEGL + STEPS
                    nth = sweep * (SEGL // 2) + STEPS // 2
                    inject(first, nth, 0)
                    with pe.Fori(0, SEGL // 2 - 1) as it:
                        pair(sweep * SEGL + it * 2 + STEPS, sweep * (SEGL // 2) + it + STEPS // 2, sweep + 1)
                    pair(sweep * SEGL + (STEPS + SEGL - 2), sweep * (SEGL // 2) + (STEPS // 2 + SEGL // 2 - 1),
                         sweep + 1, True)
                    shift_state()

            pe.wait_ge(segt, 1)
            mm(bank[6][0:SEGS, 0:D], before[0:SEGS, 0:SEGS], run, start=True, stop=True)
            mm(bank[6][0:SEGS, D:2 * D], ones[0:SEGS, 0:SEGS], run, start=True, stop=True).then_inc(segp, 1)



def kernel(**inputs):
    import numpy as np
    import concourse.bacc as bacc
    from concourse.bass_utils import run_bass_kernel_spmd as run

    def gates_first(a):
        return np.concatenate([a[2 * D:3 * D], a[0:D], a[D:2 * D], a[3 * D:4 * D]], axis=0)

    a = {k: np.asarray(val) for k, val in inputs.items()}
    consts = np.zeros((5, P, P), np.float32)
    consts[0] = np.eye(P)
    consts[1] = np.arange(P)[None, :]
    consts[2] = np.triu(np.ones((P, P)), 1)
    consts[3] = np.eye(P, k=1)
    consts[4] = 1.0
    arrays = {
        "x": a["x"], "src": a["src"], "dst": a["dst"], "edge_weight": a["edge_weight"],
        "w_gnn": a["L0_gnn_W_weight"].T, "b_gnn": a["L0_gnn_W_bias"],
        "w_ih": gates_first(a["L0_ffn_W_ih"]).T, "w_hh": gates_first(a["L0_ffn_W_hh"]).T,
        "b_ih": gates_first(a["L0_ffn_b_ih"]), "b_hh": gates_first(a["L0_ffn_b_hh"]),
        "w_lin": a["L0_ffn_W_lin"], "b_lin": a["L0_ffn_b_lin"],
        "fw": a["L0_ffn_fw_att"].reshape(D), "bw": a["L0_ffn_bw_att"].reshape(D),
        "consts": consts, "tile_iota": np.arange(TILES, dtype=np.float32),
    }
    arrays = {f"in_{k}": np.ascontiguousarray(val) for k, val in arrays.items()}
    nc = bacc.Bacc("TRN2", target_bir_lowering=False, num_devices=1)
    aps = {k[3:]: nc.dram_tensor(k, val.shape, mybir.dt.from_np(val.dtype), kind="ExternalInput").ap()
           for k, val in arrays.items()}
    out = nc.dram_tensor("out", (N, D), mybir.dt.float32, kind="ExternalOutput").ap()
    build(nc, aps, out)
    r = run(nc, [arrays], core_ids=[0])
    return r.results[0]["out"]
```

```python
from contextlib import ExitStack

import concourse.bass as bass
from concourse import mybir

N, D, E = 6250, 256, 100000
P = 128
G4 = 4 * D
H = D // 2
EP, EC = P, -(-E // P)
EMPTY = 64 * P
NB = -(-N // P)
LASTB = N - (NB - 1) * P
TILES = (E + NB * (P - 1)) // P + 1
TU = 10
TILES = -(-TILES // TU) * TU
FIRST = 9
GROUPS = (NB - FIRST) // 4
GB = TU // 2
SEGS, SEGL = 125, 50
WARM = 64
SU = 34
AB = 17
BU = 7
SHORT = (SU, 2 * SU)
CH = 5 * SU
NCH = (EC - sum(SHORT)) // CH
XPR = WARM + NB * P
TOL = 2.0 ** -19
OU = 10
EPS = 1e-5
CLOSED = -1.0e4


def build(nc, A, out, slow_sweeps=SEGS - 1, tol=TOL):
    f32, i32, u8 = mybir.dt.float32, mybir.dt.int32, mybir.dt.uint8
    u32 = mybir.dt.uint32
    bf16 = mybir.dt.bfloat16
    ALU = mybir.AluOpType
    ACT = mybir.ActivationFunctionType
    AX = mybir.AxisListType
    ds = bass.ds
    RMAX = bass.bass_isa.ReduceOp.max

    sup_d = nc.dram_tensor("support_scratch", [NB * P, D], f32).ap()
    rec_d = nc.dram_tensor("record_scratch", [P * TILES, 3], f32).ap()
    xp_d = nc.dram_tensor("gate_input_scratch", [XPR, G4], f32).ap()
    x1_d = nc.dram_tensor("x1_scratch", [NB * P, D], f32).ap()

    with ExitStack() as ctx:
        def sb(name, shape, dt=f32):
            return ctx.enter_context(nc.sbuf_tensor(name, shape, dt))

        def pb(name, shape, dt=f32):
            return ctx.enter_context(nc.psum_tensor(name, shape, dt))

        def sem(name):
            return ctx.enter_context(nc.semaphore(name))

        big_a = sb("big_a", [P, NB + 1, D])
        big_b = sb("big_b", [P, NB + 1, D])
        big_c = sb("big_c", [P, NB + 1, D])
        consts = sb("consts_sb", [P, 5, P])
        ident, iota, before, shift, ones = (consts[:, i, :] for i in range(5))
        w_gnn = sb("w_gnn", [P, 2, D])
        b_gnn = sb("b_gnn", [P, D])
        w_ih = sb("w_ih", [P, 2, G4])
        b_ih = sb("b_ih_sb", [P, G4])
        b_lin = sb("b_lin_sb", [SEGS, 2])
        b_gap = sb("b_gap", [SEGS, 1])
        fw = sb("fw", [P, D])
        bw = sb("bw", [P, D])
        records = sb("records", [P, TILES, 3])
        recs = records[:].rearrange("p t k -> p (t k)")[0:EP, 0:EC * 3].rearrange("p (c k) -> p c k", k=3)
        rec2 = records[:]
        posf = sb("posf", [EP, EC])
        cnt = sb("cnt", [EP, NB])
        pos0 = sb("pos0", [EP, NB])
        tot = sb("tot", [P, NB])
        tot_i = sb("tot_i", [P, NB], i32)
        tiles_f = sb("tiles_f", [P, NB])
        ends = sb("ends", [P, NB])
        ends_col = sb("ends_col", [NB, 1])
        table = sb("table", [1, TILES], i32)
        stg_i = sb("stg_i", [EP, 2, SU // 2], u32)
        stg_r = sb("stg_r", [EP, 2, SU // 2, 3])
        stg_g = sb("stg_g", [P, 2, TU // 2], u32)
        stg_w = sb("stg_w", [P, 2, TU // 2, 2])
        sums = sb("sums", [P, NB])
        var = sb("var", [P, NB])
        rstd = sb("rstd", [P, NB])
        tmp = sb("tmp", [P, NB])
        xn = sb("xn", [P, 2, D])
        xt = sb("xt", [P, 2, 2, P])
        pr = sb("pr", [P, 2, G4])
        gmax = sb("gmax", [P, 1])
        gall = sb("gall", [P, 1])
        flag = sb("flag", [1, 1], i32)

        spare = {"rank": big_b[:].rearrange("p b f -> p (b f)")}
        spare["later"] = big_c[:].rearrange("p b f -> p (b f)")
        taken = {"rank": 0, "later": 0}

        def part(stage, shape, dt=f32):
            size = 1
            for n in shape[1:]:
                size *= n
            at = taken[stage]
            taken[stage] += size
            view = spare[stage][0:shape[0], at:at + size]
            if dt != f32:
                view = view.bitcast(dt)
            if len(shape) == 3:
                view = view.rearrange("p (a b) -> p a b", a=shape[1])
            return view

        src_sb = part("rank", [EP, EC], i32)
        dst_sb = part("rank", [EP, EC], i32)
        bk_i = part("rank", [EP, EC], i32)
        pos_i = part("rank", [EP, EC], i32)
        w_sb = part("rank", [EP, EC])
        bk = part("rank", [EP, EC // 2]).bitcast(bf16)
        mask = part("rank", [EP, BU * EC // 2]).bitcast(bf16).rearrange("p (b c) -> p b c", b=BU)
        bk_c = part("rank", [EP, CH])
        pos_c = part("rank", [EP, CH])
        mask_c = part("rank", [EP, BU * CH // 4 + 1]).bitcast(u8)[:, 0:BU * CH].rearrange("p (b c) -> p b c", b=BU)
        cum = part("rank", [EP, BU, CH])
        pos_t = part("rank", [EP, CH], i32)
        row_t = part("rank", [EP, CH], i32)
        row_f = part("rank", [EP, CH])
        tile_iota = part("rank", [NB, TILES])
        tile_ge = part("rank", [NB, TILES])
        table_f = part("rank", [1, TILES])
        b_hh = part("later", [P, G4])
        rows = part("later", [P, TU, D])
        sign = rows.rearrange("p t f -> p (t f)")[:, 0:6 * EC // 2].bitcast(bf16).rearrange("p (b c) -> p b c", b=6)
        oneh = part("later", [P, TU, P])
        w_hh = part("later", [P, 2, G4])
        xp = part("later", [SEGS, 2, G4])
        h_s = part("later", [SEGS, 2, D])
        gc = part("later", [SEGS, 2 * 2 * 2 * H]).rearrange("p (x q s f) -> p x q s f", x=2, q=2, s=2)
        start = part("later", [SEGS, 2, D])
        h_t = part("later", [P, 2, SEGS])
        w_lin = part("later", [SEGS, 2, D])
        act_if, prod2 = (part("later", [SEGS, 2, 2 * H]) for _ in range(2))
        gap = xn[:]
        act_o = xt[0:SEGS, 0]
        act_c = xt[0:SEGS, 1]
        late = records[:].rearrange("p t k -> p (t k)")
        run, diff, base, t_h, t_s, t_o, t_w, t_d, w_gap = (late[0:SEGS, i * D:(i + 1) * D] for i in range(9))
        dot = sb("dot", [SEGS, 1])
        gate = sb("gate", [SEGS, 1])
        own = big_b[0:SEGS, 0:SEGL, :]
        x1s = big_a[0:SEGS, 0:SEGL, :]
        stats = sb("stats", [P, NB, 6])
        mean = sb("mean", [P, NB])

        bank = [pb(f"bank{i}", [P, 512]) for i in range(8)]

        load_w = sem("load_weights")
        load_c = sem("load_constants")
        load_s = sem("load_sources")
        load_e = sem("load_edges")
        load_x = sem("load_x")
        zeroed = sem("zeroed")
        rec_zero = sem("records_zeroed")
        v = sem("vector_chain")
        bk_r = sem("buckets_ready")
        signs = sem("signs_summed")
        sgn = sem("sign_scratch_free")
        counted = sem("edges_counted")
        prefixed = sem("counts_prefixed")
        ends_r = sem("bucket_ends_ready")
        ends_t = sem("ends_transposed")
        ge_done = sem("tile_compare_done")
        table_s = sem("tile_blocks_summed")
        placed = sem("edges_placed")
        staged = sem("scatter_staged")
        scat = [sem(f"scattered{i}") for i in range(2)]
        go = sem("gpsimd_may_issue")
        dgo = sem("vector_may_loop")
        pgo = sem("tensor_may_loop")
        ago = sem("scalar_may_loop")
        rec_l = sem("records_loaded")
        gst = sem("gather_staged")
        gat = [sem(f"gathered{i}") for i in range(TU)]
        oh_r = sem("onehot_ready")
        prod = sem("tile_product_done")
        added = sem("tile_added")
        var_r = sem("variance_ready")
        sq = sem("sqrt_done")
        xn_r = sem("normalised_ready")
        xt_p = sem("transposed_in_psum")
        xt_r = sem("transposed_ready")
        pj = sem("projected")
        pr_r = sem("projection_copied")
        st0 = [sem(f"projection_stored{i}") for i in range(2)]
        xn_r2 = sem("normalised2_ready")
        xt_p2 = sem("transposed2_in_psum")
        xt_r2 = sem("transposed2_ready")
        pj2 = sem("projected2")
        pr_r2 = sem("projection2_copied")
        st2 = [sem(f"projection2_stored{i}") for i in range(2)]
        x1_st = sem("x1_stored")
        x1_ld = sem("x1_by_segment_loaded")
        pad_r = sem("pad_rows_ready")
        pad_s = sem("pad_rows_stored")
        xp_l = [sem(f"gate_input_loaded{i}") for i in range(2)]
        inj = sem("gate_input_in_psum")
        g_r = [sem(f"gates_ready{x}") for x in range(2)]
        a_if = [sem(f"act_i_f_done{x}") for x in range(2)]
        a_g = [sem(f"tanh_g_done{x}") for x in range(2)]
        a_o = [sem(f"act_o_done{x}") for x in range(2)]
        a_c = [sem(f"tanh_c_done{x}") for x in range(2)]
        p_r = [sem(f"state_products_ready{x}") for x in range(2)]
        c_r = [sem(f"c_ready{x}") for x in range(2)]
        h_r = [sem(f"h_ready{x}") for x in range(2)]
        t_p = [sem(f"h_transposed_in_psum{x}") for x in range(2)]
        t_r = [sem(f"h_transposed_ready{x}") for x in range(2)]
        begun = sem("output_constants_ready")
        anew = sem("sum_begun_anew")
        dot_r = sem("logit_difference_ready")
        gate_r = sem("gate_ready")
        terms_r = sem("output_terms_ready")
        terms_u = sem("output_terms_used")
        shf = sem("state_shifted")
        gapd = sem("gap_measured")
        gapa = sem("gap_over_all")
        flg = sem("flag_ready")
        shs = sem("shift_copied")
        o_v = sem("outputs_done")
        segt = sem("segment_totals_ready")
        segp = sem("segment_prefix_done")
        res = sem("result_ready")
        out_s = sem("result_stored")

        block = ctx.enter_context(nc.Block())

        STEPS = WARM + SEGL

        @block.sync
        def _(sp):
            sp.dma_start(src_sb, A["src"].rearrange("(p c) -> p c", p=EP)).then_inc(load_s, 16)
            sp.dma_start(consts[:], A["consts"].rearrange("k p f -> p k f")).then_inc(load_c, 16)
            sp.dma_start(tile_iota, A["tile_iota"].partition_broadcast(NB)).then_inc(load_c, 16)
            sp.dma_start(dst_sb, A["dst"].rearrange("(p c) -> p c", p=EP)).then_inc(load_e, 16)
            sp.dma_start(w_sb, A["edge_weight"].rearrange("(p c) -> p c", p=EP)).then_inc(load_e, 16)
            sp.wait_ge(zeroed, 2)
            sp.dma_start(rec_d.rearrange("(p t) k -> p (t k)", p=P),
                         rec2.rearrange("p t k -> p (t k)")).then_inc(rec_zero, 16)
            sp.dma_start(big_a[:, 0:NB - 1, :], A["x"][0:(NB - 1) * P, :].rearrange("(b p) f -> p b f", p=P)
                         ).then_inc(load_x, 16)
            sp.dma_start(big_a[0:LASTB, NB - 1, :], A["x"][(NB - 1) * P:N, :]).then_inc(load_x, 16)
            for k, (name, tile) in enumerate([("w_gnn", w_gnn), ("w_ih", w_ih), ("w_hh", w_hh)]):
                sp.dma_start(tile[:, :, :], A[name].rearrange("(k p) f -> p k f", p=P)).then_inc(load_w, 16)
            sp.dma_start(b_gnn[:], A["b_gnn"].partition_broadcast(P)).then_inc(load_w, 16)
            sp.dma_start(b_ih[:], A["b_ih"].partition_broadcast(P)).then_inc(load_w, 16)
            sp.dma_start(b_hh, A["b_hh"].partition_broadcast(P)).then_inc(load_w, 16)
            sp.dma_start(w_lin, A["w_lin"].rearrange("(l f) -> l f", l=2).partition_broadcast(SEGS)
                         ).then_inc(load_w, 16)
            sp.dma_start(b_lin[:], A["b_lin"].partition_broadcast(SEGS)).then_inc(load_w, 16)
            sp.dma_start(fw[:], A["fw"].partition_broadcast(P)).then_inc(load_w, 16)
            sp.dma_start(bw[:], A["bw"].partition_broadcast(P)).then_inc(load_w, 16)

            def store_support(t, q, nth):
                first = sp.snap(t * P) if not isinstance(t, int) else t * P
                sp.wait_ge(pr_r, t + 1)
                sp.dma_start(sup_d[ds(first, P), :], pr[:, q, 0:D]).then_inc(st0[q], 16)

            with sp.Fori(0, NB // 2) as it:
                store_support(it * 2, 0, it)
                store_support(it * 2 + 1, 1, it)
            store_support(NB - 1, 0, NB // 2)

            for q in range(2):
                sp.wait_ge(scat[q], 16 * EC // 2)
            sp.dma_start(rec2.rearrange("p t k -> p (t k)"),
                         rec_d.rearrange("(p t) k -> p (t k)", p=P)).then_inc(rec_l, 16)

            sp.wait_ge(pad_r, 1)
            sp.dma_start(xp_d[0:WARM, :], pr[0:WARM, 0, :]).then_inc(pad_s, 16)

            def store_x1(t, n):
                first = sp.snap(t * P) if not isinstance(t, int) else t * P
                sp.dma_start(x1_d[ds(first, n * P), :].rearrange("(b p) f -> p b f", p=P), big_b[:, ds(t, n), :]
                             ).then_inc(x1_st, 16)

            def store_gate_input(t, q):
                first = sp.snap(t * P + WARM) if not isinstance(t, int) else t * P + WARM
                sp.wait_ge(pr_r2, t + 1)
                sp.dma_start(xp_d[ds(first, P), :], pr[:, q, :]).then_inc(st2[q], 16)

            sp.wait_ge(pad_s, 16)
            sp.wait_ge(added, TILES)
            with sp.Fori(0, NB // 2) as it:
                store_x1(it * 2, 2)
                store_gate_input(it * 2, 0)
                store_gate_input(it * 2 + 1, 1)
            store_x1(NB - 1, 1)
            store_gate_input(NB - 1, 0)
            sp.wait_ge(st2[0], 16 * (NB // 2 + 1))
            sp.wait_ge(st2[1], 16 * (NB // 2))

            def load_gate_input(u, t, q, first=False):
                row = t if isinstance(t, int) else sp.snap(t)
                if not first:
                    sp.wait_ge(inj, u - 1)
                sp.dma_start(xp[:, q, :], xp_d[ds(row, SEGS, step=SEGL), :]).then_inc(xp_l[q], 16)

            load_gate_input(0, 0, 0, True)
            load_gate_input(1, 1, 1, True)
            sp.wait_ge(x1_st, 16 * (NB // 2 + 1))
            with sp.Fori(1, SEGL // 2 + 1) as it:
                load_gate_input(it * 2, it * 2, 0)
                node = sp.snap(it * 2 - 2)
                nodes = x1_d[0:N, :].rearrange("(k l) f -> k l f", l=SEGL)[:, ds(node, 2), :]
                sp.dma_start(x1s[:, ds(node, 2), :], nodes).then_inc(x1_ld, 16)
                load_gate_input(it * 2 + 1, it * 2 + 1, 1)
            with sp.Fori(SEGL // 2 + 1, STEPS // 2) as it:
                load_gate_input(it * 2, it * 2, 0)
                load_gate_input(it * 2 + 1, it * 2 + 1, 1)
            sp.wait_ge(flg, 1)
            ok = sp.value_load(flag[0:1, 0:1], min_val=0, max_val=1)
            with sp.If(ok == 0):
                with sp.Fori(0, slow_sweeps) as sweep:
                    with sp.Fori(0, SEGL // 2) as it:
                        for q in range(2):
                            load_gate_input(sweep * SEGL + it * 2 + (STEPS + q), it * 2 + (WARM + q), q)

            for i in range(SEGL // OU):
                sp.wait_ge(res, i + 1)
                sp.dma_start(out.rearrange("(k l) f -> k l f", l=SEGL)[:, i * OU:(i + 1) * OU, :],
                             own[:, i * OU:(i + 1) * OU, :]).then_inc(out_s, 16)
            sp.wait_ge(out_s, 16 * (SEGL // OU))

        @block.gpsimd
        def _(pool):
            nc.gpsimd.memset(big_a[:, NB - 1, :], 0.0).then_inc(zeroed, 1)
            nc.gpsimd.memset(rec2, 0.0).then_inc(zeroed, 1)
            pool.wait_ge(rec_zero, 16)
            HU = SU // 2

            with pool.Fori(0, EC // SU) as it:
                for q in range(2):
                    pool.wait_ge(staged, it * 2 + (q + 1))
                    pool.sem_inc(go, 1)
                    for j in range(HU):
                        pool.indirect_dma_start(
                            out=rec_d, out_offset=bass.IndirectOffsetOnAxis(ap=stg_i[:, q, j:j + 1], axis=0),
                            in_=stg_r[:, q, j, :], in_offset=None).then_inc(scat[q], 16)

            GU = TU // 2
            for q in range(2):
                pool.wait_ge(st0[q], 16 * (NB // 2 + 1 - q))

            def gather(it):
                for q in range(2):
                    pool.wait_ge(gst, it * 2 + (q + 1))
                    pool.sem_inc(go, 1)
                    for j in range(GU):
                        s = q * GU + j
                        pool.indirect_dma_start(
                            out=rows[:, s, :], out_offset=None, in_=sup_d,
                            in_offset=bass.IndirectOffsetOnAxis(ap=stg_g[:, q, j:j + 1], axis=0)
                        ).then_inc(gat[s], 16)

            with pool.Fori(0, TILES // TU) as it:
                gather(it)

            G = nc.gpsimd

            def output(j, n):
                pool.wait_ge(terms_r, n + 1)
                if not isinstance(n, int) or n > 0:
                    pool.wait_ge(o_v, n)
                G.tensor_tensor(t_s, run, diff, ALU.mult)
                G.tensor_tensor(t_o, t_h, t_w, ALU.subtract).then_inc(terms_u, 1)
                pool.wait_ge(terms_u, n + 1)
                G.tensor_tensor(own[:, ds(j, 1), :].rearrange("k l f -> k (l f)"), t_o, t_s, ALU.add).then_inc(o_v, 1)

            pool.wait_ge(begun, 1)
            output(0, 0)
            output(1, 1)
            with pool.Fori(1, SEGL // 2) as it:
                for q in range(2):
                    output(it * 2 + q, it * 2 + q)
            pool.wait_ge(gapd, 1)
            nc.gpsimd.partition_all_reduce(gall[:], gmax[:], P, RMAX).then_inc(gapa, 1)
            pool.wait_ge(flg, 1)
            ok = pool.value_load(flag[0:1, 0:1], min_val=0, max_val=1)
            with pool.If(ok == 0):
                with pool.Fori(0, slow_sweeps) as sweep:
                    with pool.Fori(0, SEGL // 2) as it:
                        for q in range(2):
                            output(it * 2 + q, sweep * SEGL + it * 2 + (SEGL + q))

        @block.scalar
        def _(act):
            HU = SU // 2
            GU = TU // 2

            def stage_scatter(it, q, first=False):
                if not first:
                    act.wait_ge(scat[q], it * (16 * HU))
                nc.scalar.copy(stg_i[:, q, :], posf[:, ds(it * SU + q * HU, HU)])
                nc.scalar.copy(stg_r[:, q, :, :], recs[:, ds(it * SU + q * HU, HU), :]).then_inc(staged, 1)

            def sqrt_var(n, nth):
                act.wait_ge(var_r, nth)
                nc.scalar.activation(tmp[:, 0:n], var[:, 0:n], ACT.Sqrt).then_inc(sq, 1)

            def copy_transposed(t, q, ready, used, out_ready, first=False):
                act.wait_ge(ready, t + 1)
                if not first:
                    act.wait_ge(used, t - 1)
                nc.scalar.copy(xt[:, q, :, :], bank[q][:, 0:2 * P].rearrange("p (k n) -> p k n", k=2)
                               ).then_inc(out_ready, 1)

            act.wait_ge(bk_r, 1)
            for b in range(AB + 1):
                ins = nc.scalar.activation(sign[:, b % 6, :], bk, ACT.Sign, bias=tmp[:, b:b + 1],
                                           accum_out=sums[:, b:b + 1])
                if b % 6 == 5 and b < AB:
                    ins.then_inc(sgn, 1)
                    act.wait_ge(sgn, b // 6 + 1)
            ins.then_inc(signs, 1)

            def stage_chunks(first, chunks, width):
                with act.Fori(0, chunks) as c:
                    act.wait_ge(placed, c + (done[0] + 1))
                    act.sem_inc(ago, 1)
                    with act.Fori(0, width // SU) as i:
                        stage_scatter(c * (width // SU) + i + first, 0)
                        stage_scatter(c * (width // SU) + i + first, 1)
                done[0] += chunks

            act.wait_ge(placed, 1)
            stage_scatter(0, 0, True)
            stage_scatter(0, 1, True)
            done = [1]
            for k in range(1, len(SHORT)):
                stage_chunks(sum(SHORT[:k]) // SU, 1, SHORT[k])
            stage_chunks(sum(SHORT) // SU, 2, CH)
            sqrt_var(NB, 1)
            stage_chunks(sum(SHORT) // SU + 2 * (CH // SU), NCH - 2, CH)

            def stage_gather(it, q, first=False):
                if not first:
                    act.wait_ge(prod, it * TU + (q * GU + GU - TU))
                src = rec2[:, ds(it * TU + q * GU, GU), :]
                nc.scalar.copy(stg_g[:, q, :], src[:, :, 0])
                nc.scalar.copy(stg_w[:, q, :, :], src[:, :, 1:3]).then_inc(gst, 1)

            act.wait_ge(rec_l, 16)
            stage_gather(0, 0, True)
            stage_gather(0, 1, True)
            with act.Fori(1, TILES // TU) as it:
                stage_gather(it, 0)
                stage_gather(it, 1)

            sqrt_var(FIRST, 2)
            copy_transposed(0, 0, xt_p2, pj2, xt_r2, True)
            copy_transposed(1, 1, xt_p2, pj2, xt_r2, True)
            copy_transposed(2, 0, xt_p2, pj2, xt_r2)
            copy_transposed(3, 1, xt_p2, pj2, xt_r2)
            with act.Fori(0, GROUPS) as g:
                for i in range(4):
                    copy_transposed(g * 4 + (4 + i), i % 2, xt_p2, pj2, xt_r2)
                    if i == 1:
                        sqrt_var(4, g + 3)
            for t in range(4 * GROUPS + 4, NB):
                copy_transposed(t, t % 2, xt_p2, pj2, xt_r2)

            act.preload_act_table_set("sigmoid_and_others")

            def step(u, q, extra):
                def candidate(x):
                    act.wait_ge(g_r[x], u + 1)
                    nc.scalar.activation(act_if[:, x, :], bank[2 * q + x][0:SEGS, H:3 * H], ACT.Sigmoid
                                         ).then_inc(a_if[x], 1)
                    nc.scalar.activation(gc[:, x, q, 0, :], bank[2 * q + x][0:SEGS, 0:H], ACT.Tanh
                                         ).then_inc(a_g[x], 1)

                def output_gate(x):
                    nc.scalar.activation(act_o[:, x, :], bank[2 * q + x][0:SEGS, 3 * H:4 * H], ACT.Sigmoid
                                         ).then_inc(a_o[x], 1)

                def tanh_c(x):
                    act.wait_ge(c_r[x], u + 1)
                    nc.scalar.activation(act_c[:, x, :], gc[:, x, 1 - q, 1, :], ACT.Tanh).then_inc(a_c[x], 1)

                candidate(0)
                output_gate(0)
                tanh_c(0)
                candidate(1)
                output_gate(1)
                act.wait_ge(t_p[0], u + extra + 1)
                nc.scalar.copy(h_t[:, 0, :], bank[4][:, 0:SEGS]).then_inc(t_r[0], 1)
                tanh_c(1)

            with act.Fori(0, STEPS // 2) as it:
                step(it * 2, 0, 0)
                step(it * 2 + 1, 1, 0)
            act.wait_ge(flg, 1)
            ok = act.value_load(flag[0:1, 0:1], min_val=0, max_val=1)
            with act.If(ok == 0):
                with act.Fori(0, slow_sweeps) as sweep:
                    with act.Fori(0, SEGL // 2) as it:
                        for q in range(2):
                            step(sweep * SEGL + it * 2 + (STEPS + q), q, sweep + 1)

        @block.vector
        def _(dve):
            count = [0]

            def link(ins):
                count[0] += 1
                ins.then_inc(v, 1)
                dve.wait_ge(v, count[0])

            V = nc.vector
            dve.wait_ge(load_s, 16)
            link(V.tensor_scalar(bk_i, src_sb, 7, None, ALU.arith_shift_right))
            link(V.tensor_copy(bk, bk_i))
            dve.wait_ge(load_c, 32)
            V.tensor_scalar(tmp[:, 0:AB + 1], iota[:, NB - AB:NB + 1], -1.0, 0.5, ALU.mult, ALU.add).then_inc(bk_r, 1)
            for b in range(NB - AB):
                ins = V.tensor_scalar(mask[:, b % BU, :], bk, iota[:, b:b + 1], 0.0, ALU.is_equal, ALU.add,
                                      accum_out=cnt[:, b:b + 1])
                if b % BU == BU - 1 or b == NB - AB - 1:
                    link(ins)
            dve.wait_ge(signs, 1)
            link(V.tensor_tensor(cnt[:, NB - AB:NB], sums[:, 0:AB], sums[:, 1:AB + 1], ALU.subtract))
            link(V.tensor_scalar(cnt[:, NB - AB:NB], cnt[:, NB - AB:NB], 0.5, None, ALU.mult))
            dve.sem_inc(counted, 1)
            dve.wait_ge(load_e, 32)
            link(V.tensor_scalar(pos_i, src_sb, P - 1, None, ALU.bitwise_and))
            dve.wait_ge(rec_zero, 16)
            V.tensor_copy(recs[:, :, 2], pos_i)
            V.tensor_copy(recs[:, :, 1], w_sb)
            link(V.tensor_copy(recs[:, :, 0], dst_sb))
            dve.wait_ge(prefixed, 1)
            link(V.tensor_copy(tot[:], bank[0][:, 0:NB]))
            link(V.tensor_scalar(tot_i[:], tot[:], float(P - 1), None, ALU.add))
            link(V.tensor_scalar(tot_i[:], tot_i[:], 7, None, ALU.arith_shift_right))
            link(V.tensor_copy(tiles_f[:], tot_i[:]))
            link(V.tensor_tensor_scan(ends[:], tiles_f[:], tiles_f[:], 0.0, ALU.add, ALU.bypass))
            link(V.tensor_tensor(tmp[:], ends[:], tiles_f[:], ALU.subtract))
            link(V.tensor_scalar(tmp[:], tmp[:], float(P), -1.0, ALU.mult, ALU.add))
            V.tensor_tensor(pos0[:], tmp[0:EP, :], bank[1][0:EP, 0:NB], ALU.add).then_inc(ends_r, 1)
            dve.wait_ge(ends_r, 1)

            def rank(first, chunks, width):
                def wide(a):
                    return a.rearrange("p (o c) -> p o c", o=1).broadcast_to([EP, BU, width])

                def deep(a):
                    return a.rearrange("p (b o) -> p b o", o=1).broadcast_to([EP, BU, width])

                bkc, posc, post, rowt, rowf = (a[:, 0:width] for a in (bk_c, pos_c, pos_t, row_t, row_f))
                maskc, cumc = mask_c[:, :, 0:width], cum[:, :, 0:width]
                per_g = 3 + BU
                each = (NB // BU) * per_g + 6
                done = ranked[0]

                def buckets(g, n, looped):
                    V.tensor_tensor(maskc, wide(bkc), deep(iota[0:EP, ds(g * BU, BU)]), ALU.is_equal).then_inc(v, 1)
                    dve.wait_ge(v, n + 1)
                    for b in range(BU):
                        ins = V.tensor_tensor_scan(cumc[:, b, :], maskc[:, b, :], maskc[:, b, :],
                                                   pos0[:, ds(g * BU + b, 1)], ALU.add, ALU.bypass)
                    ins.then_inc(v, 1)
                    dve.wait_ge(v, n + 2)
                    V.tensor_scalar(pos0[:, ds(g * BU, BU)], cumc[:, :, width - 1], 0.0, None, ALU.add).then_inc(v, 1)
                    for b in range(BU):
                        V.copy_predicated(posc, maskc[:, b, :], cumc[:, b, :]).then_inc(v, 1)
                        dve.wait_ge(v, n + (b + 4))
                        if looped:
                            dve.sem_inc(dgo, 1)

                def chunk(c, looped):
                    m = c * each + count[0]
                    if width >= P:
                        V.tensor_scalar(posc[:, width - P:width], iota, float((TILES - 1) * P), None, ALU.add)
                    V.tensor_scalar(bkc, bk[:, ds(c * width + first, width)], 0.0, None, ALU.add).then_inc(v, 1)
                    dve.wait_ge(v, m + 1)
                    if looped:
                        dve.sem_inc(dgo, 1)
                        with dve.Fori(0, NB // BU) as g:
                            buckets(g, c * each + g * per_g + (count[0] + 1), True)
                    else:
                        for g in range(NB // BU):
                            buckets(g, m + 1 + g * per_g, False)
                    n = c * each + (count[0] + each - 5)
                    V.tensor_copy(post, posc).then_inc(v, 1)
                    dve.wait_ge(v, n + 1)
                    V.tensor_scalar(rowt, post, 7, None, ALU.arith_shift_right).then_inc(v, 1)
                    dve.wait_ge(v, n + 2)
                    V.tensor_copy(rowf, rowt).then_inc(v, 1)
                    V.tensor_scalar(post, post, P - 1, None, ALU.bitwise_and).then_inc(v, 1)
                    dve.wait_ge(v, n + 4)
                    V.scalar_tensor_tensor(posf[:, ds(c * width + first, width)], post, float(TILES), rowf,
                                           ALU.mult, ALU.add).then_inc(placed, 1)
                    dve.wait_ge(placed, c + (done + 1))
                    dve.sem_inc(v, 1)

                if chunks == 1:
                    chunk(0, False)
                else:
                    with dve.Fori(0, chunks) as c:
                        chunk(c, True)
                count[0] += each * chunks
                ranked[0] += chunks

            ranked = [0]
            for k in range(len(SHORT)):
                rank(sum(SHORT[:k]), 1, SHORT[k])
            rank(sum(SHORT), 2, CH)

            dve.wait_ge(ends_t, 1)
            link(V.tensor_copy(ends_col[:], bank[2][0:NB, 0:1]))
            V.tensor_scalar(tile_ge, tile_iota, ends_col[:, 0:1], None, ALU.is_ge).then_inc(ge_done, 1)
            dve.wait_ge(table_s, 1)
            V.tensor_scalar(table_f[0:1, 0:512], bank[3][0:1, 0:512], float(NB - 1), float(D), ALU.min, ALU.mult)
            link(V.tensor_scalar(table_f[0:1, 512:TILES], bank[4][0:1, 0:TILES - 512], float(NB - 1), float(D),
                                 ALU.min, ALU.mult))
            link(V.tensor_copy(table[:], table_f))

            LINKS = 9

            def moments(rowsin, at, slot):
                V.bn_stats(stats[:, slot, :], rowsin[:, ds(at, 1), :].rearrange("p o f -> p (o f)"))

            def variances(n, at, then):
                then(V.memset(ends_col[:], 0.0))
                even, odd = stats[:, 0:n, 1], stats[:, 0:n, 4]
                V.tensor_tensor(var[:, 0:n], stats[:, 0:n, 2], stats[:, 0:n, 5], ALU.add)
                V.tensor_tensor(tmp[:, 0:n], even, odd, ALU.add)
                then(V.tensor_tensor(sums[:, 0:n], even, odd, ALU.subtract))
                V.tensor_scalar(mean[:, ds(at, n)], tmp[:, 0:n], 0.5, None, ALU.mult)
                then(V.tensor_tensor(sums[:, 0:n], sums[:, 0:n], sums[:, 0:n], ALU.mult))
                then(V.scalar_tensor_tensor(var[:, 0:n], sums[:, 0:n], D / 4.0, var[:, 0:n], ALU.mult, ALU.add))
                V.tensor_scalar(var[:, 0:n], var[:, 0:n], 1.0 / D, EPS, ALU.mult, ALU.add).then_inc(var_r, 1)

            def scales(n, at, nth, then):
                dve.wait_ge(sq, nth)
                dve.sem_inc(dgo, 1)
                then(V.reciprocal(sums[:, 0:n], tmp[:, 0:n]))
                then(V.tensor_tensor(tmp[:, 0:n], sums[:, 0:n], sums[:, 0:n], ALU.mult))
                then(V.tensor_tensor(tmp[:, 0:n], tmp[:, 0:n], var[:, 0:n], ALU.mult))
                then(V.tensor_scalar(tmp[:, 0:n], tmp[:, 0:n], -0.5, 1.5, ALU.mult, ALU.add))
                then(V.tensor_tensor(rstd[:, ds(at, n)], sums[:, 0:n], tmp[:, 0:n], ALU.mult))

            def normalise(rowsin, t, q, ready, free, first=False):
                if not first:
                    dve.wait_ge(free, t - 1)
                V.tensor_scalar(xn[:, q:q + 1, :], rowsin[:, ds(t, 1), :], mean[:, ds(t, 1)], rstd[:, ds(t, 1)],
                                ALU.subtract, ALU.mult).then_inc(ready, 1)

            def copy_transposed(t, q):
                dve.wait_ge(xt_p, t + 1)
                V.tensor_copy(xt[:, q, :, :], bank[q][:, 0:2 * P].rearrange("p (k n) -> p k n", k=2)
                              ).then_inc(xt_r, 1)

            def evacuate_support(t, q, first=False):
                dve.wait_ge(pj, t + 1)
                if not first:
                    dve.wait_ge(st0[q], t * 8 - q * 8)
                V.tensor_tensor(pr[:, q, 0:D], bank[2 + q][:, 0:D], b_gnn[:], ALU.add).then_inc(pr_r, 1)

            dve.wait_ge(load_x, 32)
            dve.wait_ge(zeroed, 1)
            for b in range(NB):
                moments(big_a, b, b)
            variances(NB, 0, link)
            rank(sum(SHORT) + 2 * CH, NCH - 2, CH)
            scales(NB, 0, 1, link)
            link(V.tensor_copy(big_b[:, 0:NB, :], big_a[:, 0:NB, :]))
            dve.wait_ge(load_w, 16 * 10)
            V.tensor_tensor(b_ih[:], b_ih[:], b_hh, ALU.add)
            normalise(big_a, 0, 0, xn_r, xt_p, True)
            normalise(big_a, 1, 1, xn_r, xt_p, True)
            copy_transposed(0, 0)
            copy_transposed(1, 1)
            normalise(big_a, 2, 0, xn_r, xt_p)
            evacuate_support(0, 0, True)
            copy_transposed(2, 0)
            normalise(big_a, 3, 1, xn_r, xt_p)
            evacuate_support(1, 1, True)
            copy_transposed(3, 1)

            def support_pair(t):
                for q in range(2):
                    normalise(big_a, t + (q + 2), q, xn_r, xt_p)
                    evacuate_support(t + q, q)
                    copy_transposed(t + (q + 2), q)

            with dve.Fori(1, NB // 2 - 1) as it:
                support_pair(it * 2)
            normalise(big_a, NB - 1, 0, xn_r, xt_p)
            evacuate_support(NB - 3, 0)
            copy_transposed(NB - 1, 0)
            evacuate_support(NB - 2, 1)
            evacuate_support(NB - 1, 0)
            dve.wait_ge(st0[0], 16 * (NB // 2 + 1))
            dve.wait_ge(st0[1], 16 * (NB // 2))
            link(V.memset(pr[:], 0.0))
            for x in range(2):
                V.memset(pr[0:WARM, 0, (4 * x + 1) * H:(4 * x + 2) * H], CLOSED)
                ins = V.memset(pr[0:WARM, 0, (4 * x + 3) * H:(4 * x + 4) * H], CLOSED)
            ins.then_inc(pad_r, 1)

            GU = TU // 2
            regs = [dve.alloc_register(f"tile_block{s}") for s in range(TU)]
            acc = big_b[:].rearrange("p b f -> p (b f)")

            def onehots(it, q):
                dve.wait_ge(gst, it * 2 + q + 1)
                for j in range(GU):
                    s = q * GU + j
                    V.tensor_scalar(oneh[:, s, :], iota[:], stg_w[:, q, j, 1:2], stg_w[:, q, j, 0:1],
                                    ALU.is_equal, ALU.mult).then_inc(oh_r, 1)

            def add_tiles(it, q, vals):
                for j in range(GU):
                    s = q * GU + j
                    dve.wait_ge(prod, it * TU + (s + 1))
                    at = acc[:, ds(vals[s], D)]
                    V.tensor_tensor(at, at, bank[s % GB][:, 0:D], ALU.add).then_inc(added, 1)
                    dve.wait_ge(added, it * TU + (s + 1))

            onehots(0, 0)
            def blocks(it):
                dve.reg_load(regs, table[0:1, ds(it * TU, TU)])
                return [dve.snap(r, min_val=0, max_val=(NB - 1) * D) for r in regs]
            with dve.Fori(0, TILES // TU - 1) as it:
                vals = blocks(it)
                onehots(it, 1)
                add_tiles(it, 0, vals)
                onehots(it + 1, 0)
                add_tiles(it, 1, vals)
            last = TILES // TU - 1
            vals = blocks(last)
            onehots(last, 1)
            add_tiles(last, 0, vals)
            add_tiles(last, 1, vals)

            dve.wait_ge(pad_s, 16)
            for b in range(FIRST):
                moments(big_b, b, b)
            variances(FIRST, 0, link)
            scales(FIRST, 0, 2, link)

            def evacuate_gates(t, q, first=False):
                dve.wait_ge(pj2, t + 1)
                if not first:
                    dve.wait_ge(st2[q], t * 8 - q * 8)
                for c in range(2):
                    last = V.tensor_tensor(pr[:, q, c * 512:c * 512 + 512], bank[2 + 2 * q + c][:],
                                           b_ih[:, c * 512:c * 512 + 512], ALU.add)
                last.then_inc(pr_r2, 1)

            dve.wait_ge(pad_s, 16)
            normalise(big_b, 0, 0, xn_r2, xt_p2, True)
            normalise(big_b, 1, 1, xn_r2, xt_p2, True)
            normalise(big_b, 2, 0, xn_r2, xt_p2)
            evacuate_gates(0, 0, True)
            normalise(big_b, 3, 1, xn_r2, xt_p2)
            evacuate_gates(1, 1, True)

            def group(g, chain=None):
                at = g * 4 + FIRST
                for i in range(4):
                    normalise(big_b, g * 4 + (4 + i), i % 2, xn_r2, xt_p2)
                    evacuate_gates(g * 4 + (2 + i), i % 2)
                    if chain and i < 2:
                        moments(big_b, at + 2 * i, 2 * i)
                        moments(big_b, at + (2 * i + 1), 2 * i + 1)
                    if chain and i == 1:
                        variances(4, at, chain)
                    if chain and i == 2:
                        scales(4, at, g + 3, chain)

            with dve.Fori(0, GROUPS) as g:
                links = [0]

                def chain(ins):
                    links[0] += 1
                    ins.then_inc(v, 1)
                    dve.wait_ge(v, g * LINKS + (count[0] + links[0]))

                group(g, chain)
            count[0] += GROUPS * LINKS
            group(GROUPS)
            normalise(big_b, NB - 1, 0, xn_r2, xt_p2)
            evacuate_gates(NB - 3, 0)
            evacuate_gates(NB - 2, 1)
            evacuate_gates(NB - 1, 0)
            V.tensor_tensor(diff, fw[0:SEGS, :], bw[0:SEGS, :], ALU.subtract).then_inc(begun, 1)
            V.tensor_tensor(b_gap[:], b_lin[:, 0:1], b_lin[:, 1:2], ALU.subtract)
            V.tensor_tensor(w_gap, w_lin[:, 1, :], w_lin[:, 0, :], ALU.subtract)

            V.memset(gap, 0.0)
            V.memset(gc, 0.0)
            V.memset(h_t, 0.0).then_inc(t_r[0], 1)
            dve.wait_ge(t_r[0], 1)
            dve.sem_inc(t_r[1], 1)

            def copy_h(x, n):
                dve.wait_ge(t_p[x], n + 1)
                V.tensor_copy(h_t[:, x, :], bank[4 + x][:, 0:SEGS]).then_inc(t_r[x], 1)

            def step(u, q, extra, done=None, j=None):
                def products(x):
                    dve.wait_ge(a_if[x], u + 1)
                    V.tensor_tensor(prod2[:, x, H:2 * H], gc[:, x, q, 1, :], act_if[:, x, H:2 * H], ALU.mult)
                    dve.wait_ge(a_g[x], u + 1)
                    V.tensor_tensor(prod2[:, x, 0:H], gc[:, x, q, 0, :], act_if[:, x, 0:H], ALU.mult
                                    ).then_inc(p_r[x], 1)

                def new_c(x):
                    dve.wait_ge(p_r[x], u + 1)
                    V.tensor_tensor(gc[:, x, 1 - q, 1, :], prod2[:, x, 0:H], prod2[:, x, H:2 * H], ALU.add
                                    ).then_inc(c_r[x], 1)

                def new_h(x):
                    dve.wait_ge(a_c[x], u + 1)
                    V.tensor_tensor(h_s[:, q, x * H:(x + 1) * H], act_o[:, x, :], act_c[:, x, :], ALU.mult
                                    ).then_inc(h_r[x], 1)

                products(0)
                new_c(0)
                new_h(0)
                products(1)
                new_c(1)
                new_h(1)
                copy_h(1, u + extra)
                if done is not None:
                    terms(1 - q, j - 1, done - 1)

            def terms(q, j, n):
                h = h_s[:, q, :]
                if not isinstance(n, int) or n > 0:
                    dve.wait_ge(terms_u, n)
                    dve.wait_ge(terms_r, n)
                V.tensor_tensor_reduce(out=t_d, in0=h, in1=w_gap, scale=1.0, scalar=0.0, op0=ALU.mult, op1=ALU.add,
                                       accum_out=dot[:]).then_inc(dot_r, 1)
                V.scalar_tensor_tensor(t_h, h, 2.0, x1s[:, ds(j, 1), :].rearrange("k l f -> k (l f)"),
                                       ALU.mult, ALU.add)
                dve.wait_ge(dot_r, n + 1)
                V.tensor_scalar(gate[:], dot[:], b_gap[:, 0:1], None, ALU.is_gt).then_inc(gate_r, 1)
                dve.wait_ge(gate_r, n + 1)
                V.scalar_tensor_tensor(run, h, gate[:, 0:1], run, ALU.mult, ALU.add)
                V.scalar_tensor_tensor(t_w, h, gate[:, 0:1], fw[0:SEGS, :], ALU.mult, ALU.mult).then_inc(terms_r, 1)

            with dve.Fori(0, WARM // 2) as it:
                step(it * 2, 0, 0)
                step(it * 2 + 1, 1, 0)
            V.tensor_copy(start[:, 0, :], h_s[:, 1, :])
            V.tensor_copy(start[:, 1, :].rearrange("p (x f) -> p x f", x=2), gc[:, :, 0, 1, :])
            link(V.memset(run, 0.0))
            dve.wait_ge(x1_ld, 16 * (SEGL // 2))
            step(WARM, 0, 0)
            step(WARM + 1, 1, 0, 1, 1)
            with dve.Fori(1, SEGL // 2) as it:
                for q in range(2):
                    step(it * 2 + (WARM + q), q, 0, it * 2 + q, it * 2 + q)
            terms(1, SEGL - 1, SEGL - 1)

            dve.wait_ge(shf, 1)
            for k in range(2):
                ins = V.tensor_tensor(gap[0:SEGS, k, :], bank[7][0:SEGS, k * D:(k + 1) * D], start[:, k, :],
                                      ALU.subtract)
            link(ins)
            V.tensor_reduce(gmax[:], gap, AX.XY, ALU.max, apply_absolute_value=True).then_inc(gapd, 1)
            dve.wait_ge(gapa, 1)
            V.tensor_scalar(flag[:], gall[0:1, :], tol, None, ALU.is_le).then_inc(flg, 1)
            dve.wait_ge(flg, 1)
            ok = dve.value_load(flag[0:1, 0:1], min_val=0, max_val=1)
            with dve.If(ok == 0):
                with dve.Fori(0, slow_sweeps) as sweep:
                    dve.wait_ge(shf, sweep + 1)
                    dve.wait_ge(terms_r, sweep * SEGL + SEGL)
                    V.tensor_copy(h_s[:, 1, :], bank[7][0:SEGS, 0:D])
                    V.tensor_copy(gc[:, :, 0, 1, :], bank[7][0:SEGS, D:2 * D].rearrange("p (x f) -> p x f", x=2)
                                  ).then_inc(shs, 1)
                    for x in range(2):
                        copy_h(x, sweep * (SEGL + 1) + STEPS)
                    dve.wait_ge(terms_u, sweep * SEGL + SEGL)
                    V.memset(run, 0.0).then_inc(anew, 1)
                    dve.wait_ge(anew, sweep + 1)
                    u0, n0 = sweep * SEGL + STEPS, sweep * SEGL + SEGL
                    step(u0, 0, sweep + 1)
                    step(u0 + 1, 1, sweep + 1, n0 + 1, 1)
                    dve.sem_inc(dgo, 1)
                    with dve.Fori(1, SEGL // 2) as it:
                        for q in range(2):
                            step(sweep * SEGL + it * 2 + (STEPS + q), q, sweep + 1,
                                 sweep * SEGL + it * 2 + (SEGL + q), it * 2 + q)
                    terms(1, SEGL - 1, n0 + (SEGL - 1))
                dve.wait_ge(shf, slow_sweeps + 1)
                for x in range(2):
                    dve.wait_ge(t_r[x], STEPS + slow_sweeps * (SEGL + 1) + 1)
                dve.wait_ge(terms_r, SEGL * (slow_sweeps + 1))
                dve.wait_ge(o_v, SEGL * (slow_sweeps + 1))
                dve.sem_inc(dgo, 1)
            dve.wait_ge(terms_r, SEGL)
            dve.sem_inc(segt, 1)
            dve.wait_ge(o_v, SEGL)

            dve.wait_ge(segp, 1)
            V.tensor_tensor(base, bank[5][0:SEGS, D:2 * D], bw[0:SEGS, :], ALU.mult)
            link(V.tensor_tensor(t_s, bank[5][0:SEGS, 0:D], diff, ALU.mult))
            link(V.tensor_tensor(base, base, t_s, ALU.add))
            for i in range(SEGL // OU):
                part_o = own[:, i * OU:(i + 1) * OU, :]
                V.tensor_tensor(part_o, part_o, base.rearrange("k (o f) -> k o f", o=1).broadcast_to([SEGS, OU, D]),
                                ALU.add).then_inc(res, 1)

        @block.tensor
        def _(pe):
            mm = nc.tensor.matmul
            pe.wait_ge(load_c, 32)
            pe.wait_ge(counted, 1)
            mm(bank[1][0:EP, 0:NB], before[0:EP, 0:EP], cnt[:], start=True, stop=True)
            mm(bank[0][:, 0:NB], ones[0:EP, :], cnt[:], start=True, stop=True).then_inc(prefixed, 1)
            pe.wait_ge(ends_r, 1)
            mm(bank[2][0:NB, 0:1], ends[0:1, :], ones[0:1, 0:1], start=True, stop=True).then_inc(ends_t, 1)
            pe.wait_ge(ge_done, 1)
            mm(bank[3][0:1, 0:512], ones[0:NB, 0:1], tile_ge[:, 0:512], start=True, stop=True)
            mm(bank[4][0:1, 0:TILES - 512], ones[0:NB, 0:1], tile_ge[:, 512:TILES], start=True, stop=True
               ).then_inc(table_s, 1)

            def transpose_rows(t, q, ready, copied, done, first=False):
                pe.wait_ge(ready, t + 1)
                if not first:
                    pe.wait_ge(copied, t - 1)
                for k in range(2):
                    ins = nc.tensor.transpose(bank[q][:, k * P:(k + 1) * P], xn[:, q, k * P:(k + 1) * P], ident[:])
                ins.then_inc(done, 1)

            def project_support(t, q, first=False):
                pe.wait_ge(xt_r, t + 1)
                if not first:
                    pe.wait_ge(pr_r, t - 1)
                for k in range(2):
                    ins = mm(bank[2 + q][:, 0:D], xt[:, q, k, :], w_gnn[:, k, :], start=k == 0, stop=k == 1)
                ins.then_inc(pj, 1)

            def project_gates(t, q, first=False):
                pe.wait_ge(xt_r2, t + 1)
                if not first:
                    pe.wait_ge(pr_r2, t - 1)
                for c in range(2):
                    for k in range(2):
                        ins = mm(bank[2 + 2 * q + c][:], xt[:, q, k, :], w_ih[:, k, c * 512:(c + 1) * 512],
                                 start=k == 0, stop=k == 1)
                ins.then_inc(pj2, 1)

            def all_blocks(project, ready, copied, done):
                transpose_rows(0, 0, ready, copied, done, True)
                transpose_rows(1, 1, ready, copied, done, True)
                project(0, 0, True)
                transpose_rows(2, 0, ready, copied, done)
                project(1, 1, True)
                transpose_rows(3, 1, ready, copied, done)
                with pe.Fori(1, NB // 2 - 1) as it:
                    project(it * 2, 0)
                    transpose_rows(it * 2 + 2, 0, ready, copied, done)
                    project(it * 2 + 1, 1)
                    transpose_rows(it * 2 + 3, 1, ready, copied, done)
                project(NB - 3, 0)
                transpose_rows(NB - 1, 0, ready, copied, done)
                project(NB - 2, 1)
                project(NB - 1, 0)

            pe.wait_ge(load_w, 16 * 10)
            all_blocks(project_support, xn_r, xt_r, xt_p)

            def tile_products(it, first=False):
                for s in range(TU):
                    pe.wait_ge(oh_r, it * TU + (s + 1))
                    pe.wait_ge(gat[s], it * 16 + 16)
                    if not (first and s < GB):
                        pe.wait_ge(added, it * TU + (s - GB + 1))
                    mm(bank[s % GB][:, 0:D], oneh[:, s, :], rows[:, s, :], start=True, stop=True).then_inc(prod, 1)

            tile_products(0, True)
            with pe.Fori(1, TILES // TU) as it:
                tile_products(it)

            all_blocks(project_gates, xn_r2, xt_r2, xt_p2)

            def inject(q, x):
                return mm(bank[2 * q + x][0:SEGS, :], ident[0:SEGS, 0:SEGS], xp[:, q, x * 512:(x + 1) * 512],
                          start=True, stop=False)

            def inject_first(u, nth, q, first=False):
                pe.wait_ge(xp_l[q], nth * 16 + 16)
                if not first:
                    pe.wait_ge(a_o[1], u - 1)
                inject(q, 0)

            def inject_rest(q):
                inject(q, 1).then_inc(inj, 1)

            def recur(u, q, extra, late_half):
                def product(k, x, lo, hi):
                    return mm(bank[2 * q + x][0:SEGS, lo:hi], h_t[:, k, :], w_hh[:, k, x * 512 + lo:x * 512 + hi],
                              start=False, stop=k == 1)

                pe.wait_ge(t_r[0], u + extra + 1)
                product(0, 0, 0, 256)
                if late_half:
                    pe.wait_ge(h_r[1], u)
                    transpose_h(1 - q, 1)
                product(0, 0, 256, 512)
                product(0, 1, 0, 128)
                pe.wait_ge(t_r[1], u + extra + 1)
                product(1, 0, 0, 512).then_inc(g_r[0], 1)
                product(0, 1, 128, 512)
                product(1, 1, 0, 512).then_inc(g_r[1], 1)

            def transpose_h(q, x):
                nc.tensor.transpose(bank[4 + x][:, 0:SEGS], h_s[:, q, x * H:(x + 1) * H], ident[0:SEGS, 0:SEGS]
                                    ).then_inc(t_p[x], 1)

            def shift_state():
                mm(bank[7][0:SEGS, 0:D], shift[0:SEGS, 0:SEGS], h_s[:, 1, :], start=True, stop=True)
                mm(bank[7][0:SEGS, D:2 * D].rearrange("p (x f) -> p x f", x=2), shift[0:SEGS, 0:SEGS],
                   gc[:, :, 0, 1, :], start=True, stop=True).then_inc(shf, 1)

            def one(u, nth, q, extra, last=False, first=False, late_half=True):
                recur(u, q, extra, late_half)
                if not last:
                    inject_first(u + 1, nth, 1 - q, first)
                pe.wait_ge(h_r[0], u + 1)
                transpose_h(q, 0)
                if not last:
                    inject_rest(1 - q)

            def after_last(u):
                pe.wait_ge(h_r[1], u)
                transpose_h(1, 1)
                shift_state()

            pe.wait_ge(pr_r2, NB)
            inject_first(0, 0, 0, True)
            inject_rest(0)
            one(0, 0, 0, 0, first=True, late_half=False)
            one(1, 1, 1, 0)
            with pe.Fori(1, STEPS // 2 - 1) as it:
                one(it * 2, it, 0, 0)
                one(it * 2 + 1, it + 1, 1, 0)
            one(STEPS - 2, STEPS // 2 - 1, 0, 0)
            one(STEPS - 1, STEPS // 2, 1, 0, last=True)
            after_last(STEPS)
            pe.wait_ge(flg, 1)
            ok = pe.value_load(flag[0:1, 0:1], min_val=0, max_val=1)
            with pe.If(ok == 0):
                with pe.Fori(0, slow_sweeps) as sweep:
                    pe.wait_ge(shs, sweep + 1)
                    for x in range(2):
                        transpose_h(1, x)
                    u0 = sweep * SEGL + STEPS
                    m0 = sweep * (SEGL // 2) + STEPS // 2
                    inject_first(u0, m0, 0)
                    inject_rest(0)
                    one(u0, m0, 0, sweep + 1, late_half=False)
                    one(u0 + 1, m0 + 1, 1, sweep + 1)
                    pe.sem_inc(pgo, 1)
                    with pe.Fori(1, SEGL // 2 - 1) as it:
                        u, m = sweep * SEGL + it * 2 + STEPS, sweep * (SEGL // 2) + it + STEPS // 2
                        one(u, m, 0, sweep + 1)
                        one(u + 1, m + 1, 1, sweep + 1)
                    one(u0 + (SEGL - 2), m0 + (SEGL // 2 - 1), 0, sweep + 1)
                    one(u0 + (SEGL - 1), m0 + SEGL // 2, 1, sweep + 1, last=True)
                    after_last(u0 + SEGL)

            pe.wait_ge(segt, 1)
            mm(bank[5][0:SEGS, 0:D], before[0:SEGS, 0:SEGS], run, start=True, stop=True)
            mm(bank[5][0:SEGS, D:2 * D], ones[0:SEGS, 0:SEGS], run, start=True, stop=True).then_inc(segp, 1)



def kernel(**inputs):
    import numpy as np
    import concourse.bacc as bacc
    from concourse.bass_utils import run_bass_kernel_spmd as run

    def gates_first(a):
        parts = a.reshape(4, 2, H, *a.shape[1:])
        return parts[[2, 0, 1, 3]].swapaxes(0, 1).reshape(a.shape)

    def edges(name, empty):
        laid = np.full(EP * EC, empty, a[name].dtype)
        laid[:E] = a[name]
        return laid

    a = {k: np.asarray(val) for k, val in inputs.items()}
    consts = np.zeros((5, P, P), np.float32)
    consts[0] = np.eye(P)
    consts[1] = np.arange(P)[None, :]
    consts[2] = np.triu(np.ones((P, P)), 1)
    consts[3] = np.eye(P, k=1)
    consts[4] = 1.0
    arrays = {
        "x": a["x"], "src": edges("src", EMPTY), "dst": edges("dst", 0), "edge_weight": edges("edge_weight", 0),
        "w_gnn": a["L0_gnn_W_weight"].T, "b_gnn": a["L0_gnn_W_bias"],
        "w_ih": gates_first(a["L0_ffn_W_ih"]).T, "w_hh": gates_first(a["L0_ffn_W_hh"]).T,
        "b_ih": gates_first(a["L0_ffn_b_ih"]), "b_hh": gates_first(a["L0_ffn_b_hh"]),
        "w_lin": a["L0_ffn_W_lin"].reshape(2 * D), "b_lin": a["L0_ffn_b_lin"],
        "fw": a["L0_ffn_fw_att"].reshape(D), "bw": a["L0_ffn_bw_att"].reshape(D),
        "consts": consts, "tile_iota": np.arange(TILES, dtype=np.float32),
    }
    arrays = {f"in_{k}": np.ascontiguousarray(val) for k, val in arrays.items()}
    nc = bacc.Bacc("TRN2", target_bir_lowering=False, num_devices=1)
    aps = {k[3:]: nc.dram_tensor(k, val.shape, mybir.dt.from_np(val.dtype), kind="ExternalInput").ap()
           for k, val in arrays.items()}
    out = nc.dram_tensor("out", (N, D), mybir.dt.float32, kind="ExternalOutput").ap()
    build(nc, aps, out)
    r = run(nc, [arrays], core_ids=[0])
    return r.results[0]["out"]
```
